# Optimizing a Trainium2 kernel written in Bass

```python
import numpy as np
import jax
import jax.numpy as jnp

def _softmax(x, axis=-1):
    return jax.nn.softmax(x, axis=axis)

def _gelu(x):
    return jax.nn.gelu(x, approximate=True)

def _silu(x):
    return jax.nn.silu(x)

def _sigmoid(x):
    return jax.nn.sigmoid(x)

def _layernorm(x, axis=-1, eps=1e-05):
    m = jnp.mean(x, axis=axis, keepdims=True)
    v = jnp.var(x, axis=axis, keepdims=True)
    return (x - m) / jnp.sqrt(v + eps)

def _scatter_add(tgt, idx, src, axis=0):
    return tgt.at[idx].add(src)

def _segment_sum(src, seg, n):
    return jax.ops.segment_sum(src, seg, n)
kernel_name = 'mk_prb_d1_jaxref_r8_fafdae'

def setup_inputs(seed: int=0):
    np.random.seed(seed)
    _w = jnp.asarray

    def _L0_attn_setup():
        import jax, jax.numpy as jnp
        import numpy as np
        import math
        FEATURE_DIM = 16
        NUM_HEADS = 16
        HIDDEN = 128
        HEAD_DIM = HIDDEN // NUM_HEADS
        EPS = 1e-12
        IU, JU = np.triu_indices(FEATURE_DIM, 1)
        RD = math.sqrt(FEATURE_DIM)
        RRD = math.sqrt(RD)
        R2 = math.sqrt(2.0)

        def taylor_feature_map(x):
            x2 = x[..., :, None] * x[..., None, :]
            off = x2[..., IU, JU]
            diag = jnp.square(x)
            ones = jnp.ones_like(x[..., :1])
            return jnp.concatenate([ones, x / RRD, diag / (RD * R2), off / RD], axis=-1)
        key = jax.random.key(seed)
        k0, k1, k2, k3, k4 = jax.random.split(key, 5)
        b, t = (2, 64)
        s = 1.0 / math.sqrt(HIDDEN)
        return {'hidden_states': jax.random.normal(k0, (b, t, HIDDEN), jnp.float32), 'Wq': jax.random.normal(k1, (NUM_HEADS * FEATURE_DIM, HIDDEN), jnp.float32) * s, 'Wk': jax.random.normal(k2, (NUM_HEADS * FEATURE_DIM, HIDDEN), jnp.float32) * s, 'Wv': jax.random.normal(k3, (HIDDEN, HIDDEN), jnp.float32) * s, 'Wo': jax.random.normal(k4, (HIDDEN, HIDDEN), jnp.float32) * s}
    _L0_attn_in = _L0_attn_setup()

    def _L0_ffn_setup():
        import jax, jax.numpy as jnp
        import numpy as np
        B, F, D, H, E, K = (4, 256, 128, 256, 8, 2)
        key = jax.random.key(seed)
        ks = jax.random.split(key, 9)
        sc = lambda k, shape, fan_in: jax.random.normal(k, shape, jnp.float32) * fan_in ** (-0.5)
        return {'x': jax.random.normal(ks[0], (B, F, D), jnp.float32), 'rw1': sc(ks[1], (D, D), D), 'rb1': jnp.zeros((D,), jnp.float32), 'rw2': sc(ks[2], (D, E), D), 'rb2': jnp.zeros((E,), jnp.float32), 'ew1': sc(ks[3], (E, D, H), D), 'eb1': jnp.zeros((E, H), jnp.float32), 'ew2': sc(ks[4], (E, H, D), H), 'eb2': jnp.zeros((E, D), jnp.float32)}
    _L0_ffn_in = _L0_ffn_setup()
    _d = {'L0_attn_hidden_states': _L0_attn_in['hidden_states'], 'L0_attn_Wq': _L0_attn_in['Wq'], 'L0_attn_Wk': _L0_attn_in['Wk'], 'L0_attn_Wv': _L0_attn_in['Wv'], 'L0_attn_Wo': _L0_attn_in['Wo'], 'L0_ffn_rw1': _L0_ffn_in['rw1'], 'L0_ffn_rb1': _L0_ffn_in['rb1'], 'L0_ffn_rw2': _L0_ffn_in['rw2'], 'L0_ffn_rb2': _L0_ffn_in['rb2'], 'L0_ffn_ew1': _L0_ffn_in['ew1'], 'L0_ffn_eb1': _L0_ffn_in['eb1'], 'L0_ffn_ew2': _L0_ffn_in['ew2'], 'L0_ffn_eb2': _L0_ffn_in['eb2']}
    _x0 = _d['L0_attn_hidden_states']
    _d['L0_attn_hidden_states'] = jax.random.normal(jax.random.fold_in(jax.random.key(seed), 1), (8, 256, 128), dtype=_x0.dtype)
    del _x0
    return _d

def reference(L0_attn_hidden_states, L0_attn_Wq, L0_attn_Wk, L0_attn_Wv, L0_attn_Wo, L0_ffn_rw1, L0_ffn_rb1, L0_ffn_rw2, L0_ffn_rb2, L0_ffn_ew1, L0_ffn_eb1, L0_ffn_ew2, L0_ffn_eb2):

    def _L0_attn_ref(hidden_states, Wq, Wk, Wv, Wo):
        import jax, jax.numpy as jnp
        import numpy as np
        import math
        FEATURE_DIM = 16
        NUM_HEADS = 16
        HIDDEN = 128
        HEAD_DIM = HIDDEN // NUM_HEADS
        EPS = 1e-12
        IU, JU = np.triu_indices(FEATURE_DIM, 1)
        RD = math.sqrt(FEATURE_DIM)
        RRD = math.sqrt(RD)
        R2 = math.sqrt(2.0)

        def taylor_feature_map(x):
            x2 = x[..., :, None] * x[..., None, :]
            off = x2[..., IU, JU]
            diag = jnp.square(x)
            ones = jnp.ones_like(x[..., :1])
            return jnp.concatenate([ones, x / RRD, diag / (RD * R2), off / RD], axis=-1)
        b, t, _ = hidden_states.shape
        q = (hidden_states @ Wq.T).reshape(b, t, NUM_HEADS, FEATURE_DIM).transpose(0, 2, 1, 3)
        k = (hidden_states @ Wk.T).reshape(b, t, NUM_HEADS, FEATURE_DIM).transpose(0, 2, 1, 3)
        v = (hidden_states @ Wv.T).reshape(b, t, NUM_HEADS, HEAD_DIM).transpose(0, 2, 1, 3)
        q = taylor_feature_map(q)
        k = taylor_feature_map(k)
        kv = jnp.cumsum(k[..., None, :] * v[..., :, None], axis=2)
        y = jnp.einsum('bhtD,bhtdD->bhtd', q, kv)
        z = jnp.cumsum(k, axis=2)
        denom = jnp.sum(q * z, axis=-1, keepdims=True) + EPS
        y = y / denom
        y = y.transpose(0, 2, 1, 3).reshape(b, t, NUM_HEADS * HEAD_DIM)
        return y @ Wo.T

    def _L0_ffn_ref(x, rw1, rb1, rw2, rb2, ew1, eb1, ew2, eb2):
        import jax, jax.numpy as jnp
        import numpy as np
        B, F, D, H, E, K = (4, 256, 128, 256, 8, 2)
        b, f, d = x.shape
        t = x.reshape(b * f, d)
        logits = jax.nn.silu(t @ rw1 + rb1) @ rw2 + rb2
        vals, idx = jax.lax.top_k(logits, K)
        rows = jnp.arange(t.shape[0])[:, None]
        masked = jnp.full_like(logits, -jnp.inf).at[rows, idx].set(vals)
        w = jax.nn.softmax(masked, axis=1)
        eh = jax.nn.silu(jnp.einsum('td,edh->teh', t, ew1) + eb1[None])
        eo = jnp.einsum('teh,ehd->ted', eh, ew2) + eb2[None]
        y = t + jnp.einsum('te,ted->td', w, eo)
        return y.reshape(b, f, d)
    x = L0_attn_hidden_states
    xn = _layernorm(x, axis=-1)
    x = x + _L0_attn_ref(xn, L0_attn_Wq, L0_attn_Wk, L0_attn_Wv, L0_attn_Wo) + _L0_ffn_ref(xn, L0_ffn_rw1, L0_ffn_rb1, L0_ffn_rw2, L0_ffn_rb2, L0_ffn_ew1, L0_ffn_eb1, L0_ffn_ew2, L0_ffn_eb2)
    return x

_drawn_inputs = setup_inputs


def setup_inputs(seed=0):
    import zlib

    import numpy as np

    out = dict(_drawn_inputs(seed))
    spreads = {'L0_ffn_rb1': (0.0, 0.1),
     'L0_ffn_rb2': (0.0, 0.1),
     'L0_ffn_eb1': (0.0, 0.377),
     'L0_ffn_eb2': (0.0, 0.1)}
    factors = {}
    for name, (base, spread) in spreads.items():
        noise = np.random.default_rng([zlib.crc32(name.encode()), seed]).standard_normal(out[name].shape)
        drawn = base * np.exp(spread * noise) if base else spread * noise
        out[name] = jnp.asarray(drawn.astype(out[name].dtype))
    for name, factor in factors.items():
        out[name] = (out[name] * factor).astype(out[name].dtype)
    return out
```

```python
from contextlib import ExitStack

import concourse.bass as bass
from concourse import mybir

F32 = mybir.dt.float32
F32R = mybir.dt.float32r
I32 = mybir.dt.int32
U32 = mybir.dt.uint32
ALU = mybir.AluOpType
ACT = mybir.ActivationFunctionType

P = 128
RD = 4.0
EPS_LN = 1e-5
EPS_DEN = 1e-12


def fused_layer(nc, x, wqT, wkT, wvT, woT, rw1, rb1, rw2, rb2, ew1, eb1, ew2, eb2, out):
    B, TB, D = x.shape
    NT = TB // P
    TILES = B * NT
    FD = 16
    H = wqT.shape[1] // FD
    HD = D // H
    HD1 = HD + 1
    E, _, HID = ew1.shape
    NC = HID // P
    PAIRS = H // 2
    QC = H // 4
    SW = TB + P
    assert D == P and NT == 2 and PAIRS == E and NC == 2

    x_v = x.rearrange("b (t p) d -> p (b t) d", p=P)
    out_v = out.rearrange("b (t p) d -> p (b t) d", p=P)

    with ExitStack() as ctx:
        def sb(name, shape, dt=F32):
            return ctx.enter_context(nc.sbuf_tensor(name, shape, dt))

        def sem(name):
            return ctx.enter_context(nc.semaphore(name))

        ident = sb("ident", [P, P])
        causal = sb("causal", [P, P])
        ones = sb("ones", [P, P])
        iota8 = sb("iota8", [P, E])
        part_i = sb("part_i", [P, 1], I32)
        part_b = sb("part_b", [P, 1], I32)
        neg_lo = sb("neg_lo", [P, 1])
        wq_f = sb("wq_f", [P, H * FD])
        wk_f = sb("wk_f", [P, H * FD])
        wv_f = sb("wv_f", [P, D])
        wo_f = sb("wo_f", [P, D])
        rw1_f = sb("rw1_f", [P, D])
        rw2_f = sb("rw2_f", [P, E])
        rb1_c = sb("rb1_c", [P, 1])
        rb2_r = sb("rb2_r", [1, E])
        eb1_c = sb("eb1_c", [P, E * NC])
        eb2_r = sb("eb2_r", [E, D])
        ew1_f = sb("ew1_f", [P, E, HID])
        ew2_f = sb("ew2_f", [P, E * NC, D])
        wqk_hi = sb("wqk_hi", [P, 2, H, 2, FD], F32R)
        wqk_lo = sb("wqk_lo", [P, 2, H, 2, FD], F32R)
        wv_hi = sb("wv_hi", [P, D], F32R)
        wv_lo = sb("wv_lo", [P, D], F32R)
        rw1_hi = sb("rw1_hi", [P, D], F32R)
        rw1_lo = sb("rw1_lo", [P, D], F32R)
        ew1_hi = sb("ew1_hi", [P, E, HID], F32R)
        ew1_lo = sb("ew1_lo", [P, E, HID], F32R)
        ew2_hi = sb("ew2_hi", [P, E * NC, D], F32R)
        ew2_lo = sb("ew2_lo", [P, E * NC, D], F32R)

        x_all = sb("x_all", [P, TILES, D])
        stats = sb("stats", [P, TILES, 6])
        mv = sb("mv", [P, TILES, 2])
        var_eps = sb("var_eps", [P, TILES])
        inv_var = sb("inv_var", [P, TILES])
        rstd0 = sb("rstd0", [P, TILES])
        newton = sb("newton", [P, TILES])
        rstd = sb("rstd", [P, TILES])
        xn = sb("xn", [P, 2, NT, D])
        acc = sb("acc", [P, 2, NT, D])
        xT_hi = sb("xT_hi", [P, 2, TB], F32R)
        xT_lo = sb("xT_lo", [P, 2, TB], F32R)
        qk_hi = sb("qk_hi", [P, 2, QC, 2, TB], F32R)
        q_mix = sb("q_mix", [P, 2, QC, TB], F32R)
        k_lo = sb("k_lo", [P, 2, QC, TB], F32R)
        v_aug = sb("v_aug", [P, 2, NT, H, HD1])
        r1T = sb("r1T", [P, 2, TB])
        gate = sb("gate", [P, 2, NT, E])
        w_att = sb("w_att", [P, 2, 2, SW])
        h_f = sb("h_f", [P, 2, NC, TB])
        h_hi = sb("h_hi", [P, 2, NC, TB], F32R)
        h_lo = sb("h_lo", [P, 2, NC, TB], F32R)
        lg = sb("lg", [P, NT, E])
        top = sb("top", [P, NT, 8])
        topi = sb("topi", [P, NT, 8], U32)
        topf = sb("topf", [P, NT, 2])
        gap = sb("gap", [P, NT])
        th = sb("th", [P, NT])
        w12 = sb("w12", [P, NT, 2])
        hot = sb("hot", [P, NT, 2, E])
        hotw = sb("hotw", [P, NT, 2, E])
        den = sb("den", [P, NT * H])
        rden = sb("rden", [P, NT * H])
        y = sb("y", [P, NT, D])
        yT = sb("yT", [P, TB])
        gateT = sb("gateT", [E, TB])

        ps_s = ctx.enter_context(nc.psum_tensor("ps_s", [P, 2, 512], F32))
        ps_h = ctx.enter_context(nc.psum_tensor("ps_h", [P, NC, TB], F32))
        ps_e = ctx.enter_context(nc.psum_tensor("ps_e", [P, NT, 256], F32))
        ps_num = ctx.enter_context(nc.psum_tensor("ps_num", [P, 512], F32))
        ps_t = ctx.enter_context(nc.psum_tensor("ps_t", [P, 512], F32))
        ps_qk = ctx.enter_context(nc.psum_tensor("ps_qk", [P, 2, TB], F32))
        ps_y = ctx.enter_context(nc.psum_tensor("ps_y", [P, 2, TB], F32))
        NUMW = H * HD1

        x_in = [sem(f"x_in{g}") for g in range(4)]
        wqkvr_in = sem("wqkvr_in")
        small_in = sem("small_in")
        ew1_in = sem("ew1_in")
        ew2_in = sem("ew2_in")
        const_step = sem("const_step")
        neg_lo_ready = sem("neg_lo_ready")
        v_ones = sem("v_ones")
        w_split = sem("w_split")
        ew1_hi_done = sem("ew1_hi_done")
        ew1_lo_done = sem("ew1_lo_done")
        ew2_hi_done = sem("ew2_hi_done")
        ew2_lo_done = sem("ew2_lo_done")
        ln_step = sem("ln_step")
        sqrt_done = sem("sqrt_done")
        xn_ready = sem("xn_ready")
        residual_ready = sem("residual_ready")
        xT_psum = sem("xT_psum")
        xT_hi_done = sem("xT_hi_done")
        xT_lo_done = sem("xT_lo_done")
        v_psum = sem("v_psum")
        v_ready = sem("v_ready")
        qk_psum = sem("qk_psum")
        qk_hi_done = sem("qk_hi_done")
        qk_lo_done = sem("qk_lo_done")
        r1_psum = sem("r1_psum")
        r1_ready = sem("r1_ready")
        lg_psum = sem("lg_psum")
        lg_read = sem("lg_read")
        route_step = sem("route_step")
        tanh_done = sem("tanh_done")
        gate_ready = sem("gate_ready")
        s_psum = sem("s_psum")
        square_done = sem("square_done")
        mask_done = sem("mask_done")
        pv_done = sem("pv_done")
        h_psum = sem("h_psum")
        silu_done = sem("silu_done")
        h_hi_done = sem("h_hi_done")
        h_lo_done = sem("h_lo_done")
        e_psum = sem("e_psum")
        moe_added = sem("moe_added")
        den_step = sem("den_step")
        y_ready = sem("y_ready")
        yT_psum = sem("yT_psum")
        yT_ready = sem("yT_ready")
        att_psum = sem("att_psum")
        out_ready = sem("out_ready")
        out_stored = sem("out_stored")

        ROUTE_STEPS = 9
        CONST_ALL = 9
        W_ATT_SPLIT = 12

        def for_batches(eng, batch):
            batch(0, 0, True)
            with eng.Fori(0, B // 2 - 1) as i:
                batch(i * 2 + 1, 1, True)
                batch(i * 2 + 2, 0, True)
            batch(B - 1, 1, False)

        def wait_used(eng, what, n):
            if not isinstance(n, int) or n > 0:
                eng.wait_ge(what, n)

        block = ctx.enter_context(nc.Block())

        @block.sync
        def _(sp):
            for g in range(4):
                n = TILES // 4
                sp.dma_start(x_all[:, g * n:(g + 1) * n, :], x_v[:, g * n:(g + 1) * n, :]).then_inc(x_in[g], 16)
            sp.dma_start(ew1_f[:, :, :], ew1.rearrange("e d h -> d e h")).then_inc(ew1_in, 16)
            sp.dma_start(ew2_f[:, :, :], ew2.rearrange("e (c p) d -> p (e c) d", p=P)).then_inc(ew2_in, 16)

            def store(b, r, _):
                sp.wait_ge(out_ready, b + 1)
                sp.dma_start(out_v[:, bass.ds(b * NT, NT), :], acc[:, r, :, :]).then_inc(out_stored, 16)

            for_batches(sp, store)
            sp.wait_ge(out_stored, 16 * B)

        @block.gpsimd
        def _(pool):
            pool.memset(ident[:, :], 0.0).then_inc(const_step, 1)
            pool.memset(causal[:, :], 1.0).then_inc(const_step, 1)
            pool.memset(ones[:, :], 1.0).then_inc(const_step, 1)
            pool.iota(part_i[:, :], pattern=[[0, 1]], base=0, channel_multiplier=1).then_inc(const_step, 1)
            pool.iota(iota8[:, :], pattern=[[1, E]], base=0, channel_multiplier=0,
                      allow_small_or_imprecise_dtypes=True).then_inc(const_step, 1)
            pool.wait_ge(const_step, 5)
            pool.affine_select(out=ident[:, :], in_=ident[:, :], compare_op=ALU.not_equal, fill=1.0,
                               base=0, pattern=[[-1, P]], channel_multiplier=1).then_inc(const_step, 1)
            pool.affine_select(out=causal[:, :], in_=causal[:, :], compare_op=ALU.is_ge, fill=0.0,
                               base=0, pattern=[[1, P]], channel_multiplier=-1).then_inc(const_step, 1)
            for r in range(2):
                pool.memset(v_aug[:, r, :, :, HD:HD1], 1.0).then_inc(const_step, 1)

            def residual(b, r):
                pool.wait_ge(xn_ready, NT * (b + 1))
                pool.tensor_tensor(acc[:, r, :, :], x_all[:, bass.ds(b * NT, NT), :], xn[:, r, :, :],
                                   ALU.add).then_inc(residual_ready, 1)

            residual(0, 0)
            for e in range(E):
                pool.wait_ge(ew1_hi_done, e + 1)
                pool.tensor_tensor(ew1_lo[:, e, :], ew1_f[:, e, :], ew1_hi[:, e, :].bitcast(F32),
                                   ALU.subtract).then_inc(ew1_lo_done, 1)
                pool.wait_ge(ew2_hi_done, e + 1)
                pool.tensor_tensor(ew2_lo[:, NC * e:NC * (e + 1), :], ew2_f[:, NC * e:NC * (e + 1), :],
                                   ew2_hi[:, NC * e:NC * (e + 1), :].bitcast(F32),
                                   ALU.subtract).then_inc(ew2_lo_done, 1)

            def batch(b, r, has_next):
                for k in range(PAIRS):
                    if k == 1 and has_next:
                        wait_used(pool, out_stored, b * 16)
                        residual(b + 1, 1 - r)
                    pool.wait_ge(square_done, b * PAIRS + (k + 1))
                    pool.nop(nofuse=True)
                    for j in range(2):
                        diag = w_att[:, k % 2, j, :].rearrange("p (n q) -> p n q", q=P)[:, 0:3:2, :]
                        last = pool.affine_select(out=diag, in_=diag, compare_op=ALU.is_ge, fill=0.0, base=0,
                                                  pattern=[[0, 2], [1, P]], channel_multiplier=-1)
                    last.then_inc(mask_done, 1)

            for_batches(pool, batch)

        @block.scalar
        def _(act):
            for dst, src in ((wq_f, wqT), (wk_f, wkT), (wv_f, wvT), (rw1_f, rw1)):
                act.dma_start(dst[:, :], src).then_inc(wqkvr_in, 16)
            for dst, src in ((rb1_c, rb1), (rw2_f, rw2), (rb2_r, rb2), (eb1_c, eb1), (wo_f, woT), (eb2_r, eb2)):
                act.dma_start(dst[:, :], src).then_inc(small_in, 16)
            act.wait_ge(ln_step, 3)
            act.activation(rstd0[:, :], inv_var[:, :], ACT.Sqrt).then_inc(sqrt_done, 1)

            def split_hi(e):
                act.activation(ew1_hi[:, e, :], ew1_f[:, e, :], ACT.Copy).then_inc(ew1_hi_done, 1)
                act.activation(ew2_hi[:, NC * e:NC * (e + 1), :], ew2_f[:, NC * e:NC * (e + 1), :],
                               ACT.Copy).then_inc(ew2_hi_done, 1)

            def xT(b, r):
                act.wait_ge(xT_psum, b + 1)
                act.activation(xT_hi[:, r, :], ps_t[:, 0:TB], ACT.Copy).then_inc(xT_hi_done, 1)

            def qk(b, r, c):
                act.wait_ge(qk_psum, b * QC + (c + 1))
                act.activation(qk_hi[:, r, c, :, :], ps_qk[:, :, :], ACT.Copy).then_inc(qk_hi_done, 1)

            def v(b, r):
                act.wait_ge(v_psum, b + 1)
                act.activation(v_aug[:, r, :, :, 0:HD].rearrange("p t h d -> p (t h) d"),
                               ps_t[:, 0:TB].rearrange("p (n d) -> p n d", d=HD), ACT.Copy).then_inc(v_ready, 1)

            def r1(b, r):
                act.wait_ge(r1_psum, b + 1)
                act.activation(r1T[:, r, :], ps_t[:, 0:TB], ACT.Silu, bias=rb1_c[:, 0:1]).then_inc(r1_ready, 1)

            def tanh(b, r):
                act.wait_ge(route_step, b * ROUTE_STEPS + 7)
                act.activation(th[:, :], gap[:, :], ACT.Tanh, scale=0.5).then_inc(tanh_done, 1)

            act.wait_ge(small_in, 16 * 6)
            xT(0, 0)
            v(0, 0)
            for c in range(QC):
                qk(0, 0, c)
            r1(0, 0)
            act.wait_ge(ew1_in, 16)
            act.wait_ge(ew2_in, 16)
            for e in range(E):
                split_hi(e)
            tanh(0, 0)

            def square(b, k):
                act.wait_ge(s_psum, b * PAIRS + (k + 1))
                wait_used(act, pv_done, b * PAIRS + max(k - 1, 0))
                act.activation(w_att[:, k % 2, :, :], ps_s[:, :, 0:SW], ACT.Square, bias=1.0,
                               scale=1.0 / RD).then_inc(square_done, 1)

            def silu(b, e):
                act.wait_ge(h_psum, b * E + (e + 1))
                wait_used(act, h_lo_done, b * E + max(e - 1, 0))
                for c in range(NC):
                    last = act.activation(h_f[:, e % 2, c, :], ps_h[:, c, :], ACT.Silu,
                                          bias=eb1_c[:, e * NC + c:e * NC + c + 1])
                last.then_inc(silu_done, 1)

            def batch(b, r, has_next):
                for k in range(PAIRS):
                    square(b, k)
                    if has_next:
                        if k == 1:
                            xT(b + 1, 1 - r)
                        if k == 2:
                            v(b + 1, 1 - r)
                        if 2 <= k < 2 + QC:
                            qk(b + 1, 1 - r, k - 2)
                        if k == 5:
                            r1(b + 1, 1 - r)
                        if k == 7:
                            tanh(b + 1, 1 - r)
                    silu(b, k)
                act.wait_ge(yT_psum, b + 1)
                wait_used(act, att_psum, b)
                act.activation(yT[:, :], ps_y[:, 0, :], ACT.Copy)
                act.activation(gateT[:, :], ps_y[0:E, 1, :], ACT.Copy).then_inc(yT_ready, 1)

            for_batches(act, batch)

        @block.vector
        def _(dve):
            for g in range(4):
                dve.wait_ge(x_in[g], 16)
                for t in range(g * TILES // 4, (g + 1) * TILES // 4):
                    last = dve.bn_stats(stats[:, t, :], x_all[:, t, :])
            last.then_inc(ln_step, 1)
            dve.wait_ge(ln_step, 1)
            for t in range(TILES):
                last = dve.bn_aggr(mv[:, t, :], stats[:, t, :])
            last.then_inc(den_step, 1)
            dve.wait_ge(den_step, 1)
            dve.tensor_scalar(var_eps[:, :], mv[:, :, 1], EPS_LN, None, ALU.add).then_inc(ln_step, 1)
            dve.wait_ge(ln_step, 2)
            dve.reciprocal(inv_var[:, :], var_eps[:, :]).then_inc(ln_step, 1)
            dve.wait_ge(sqrt_done, 1)
            dve.tensor_tensor(newton[:, :], rstd0[:, :], rstd0[:, :], ALU.mult).then_inc(ln_step, 1)
            dve.wait_ge(ln_step, 4)
            dve.tensor_tensor(newton[:, :], newton[:, :], var_eps[:, :], ALU.mult).then_inc(ln_step, 1)
            dve.wait_ge(ln_step, 5)
            dve.tensor_scalar(newton[:, :], newton[:, :], -0.5, 1.5, ALU.mult, ALU.add).then_inc(ln_step, 1)
            dve.wait_ge(ln_step, 6)
            dve.tensor_tensor(rstd[:, :], rstd0[:, :], newton[:, :], ALU.mult).then_inc(ln_step, 1)
            dve.wait_ge(ln_step, 7)

            def normalise(b, r):
                for t in range(NT):
                    dve.tensor_scalar(xn[:, r, t, :], x_all[:, bass.ds(b * NT + t, 1), :].squeeze(1),
                                      mv[:, bass.ds(b * NT + t, 1), 0:1].squeeze(1),
                                      rstd[:, bass.ds(b * NT + t, 1)],
                                      ALU.subtract, ALU.mult).then_inc(xn_ready, 1)

            normalise(0, 0)
            dve.wait_ge(wqkvr_in, 16 * 4)
            pairs = [(wqk_hi[:, m, :, c, :], wqk_lo[:, m, :, c, :], w[:, :].rearrange("p (h f) -> p h f", f=FD))
                     for m, w in enumerate((wq_f, wk_f)) for c in range(2)]
            pairs += [(wv_hi[:, :], wv_lo[:, :], wv_f[:, :]), (rw1_hi[:, :], rw1_lo[:, :], rw1_f[:, :])]
            for hi, lo, w in pairs:
                dve.tensor_copy(hi, w).then_inc(w_split, 1)
            for n, (hi, lo, w) in enumerate(pairs):
                dve.wait_ge(w_split, len(pairs))
                dve.tensor_tensor(lo, w, hi.bitcast(F32), ALU.subtract).then_inc(w_split, 1)
            dve.wait_ge(const_step, CONST_ALL)
            dve.tensor_scalar(part_b[:, :], part_i[:, :], 4, 1, ALU.logical_shift_right,
                              ALU.bitwise_and).then_inc(neg_lo_ready, 1)
            dve.wait_ge(neg_lo_ready, 1)
            dve.tensor_scalar(neg_lo[:, :], part_b[:, :], -1.0, None, ALU.mult).then_inc(neg_lo_ready, 1)
            dve.wait_ge(neg_lo_ready, 2)

            def xT(b, r):
                dve.wait_ge(xT_hi_done, b + 1)
                dve.tensor_tensor(xT_lo[:, r, :], ps_t[:, 0:TB], xT_hi[:, r, :].bitcast(F32),
                                  ALU.subtract).then_inc(xT_lo_done, 1)

            def qk(b, r, c):
                dve.wait_ge(qk_hi_done, b * QC + (c + 1))
                dve.scalar_tensor_tensor(out=q_mix[:, r, c, :], in0=qk_hi[:, r, c, 0, :].bitcast(F32),
                                         scalar=neg_lo[:, 0:1], in1=ps_qk[:, 0, :], op0=ALU.mult, op1=ALU.add)
                dve.tensor_tensor(k_lo[:, r, c, :], ps_qk[:, 1, :], qk_hi[:, r, c, 1, :].bitcast(F32),
                                  ALU.subtract).then_inc(qk_lo_done, 1)

            def route(b, r):
                def step(n):
                    dve.wait_ge(route_step, b * ROUTE_STEPS + n)

                dve.wait_ge(lg_psum, b + 1)
                dve.tensor_copy(lg[:, :, :].rearrange("p t e -> p (t e)"), ps_t[:, 0:NT * E]).then_inc(lg_read, 1)
                dve.wait_ge(lg_read, b + 1)
                dve.nop(nofuse=True)
                for t in range(NT):
                    dve.max(top[:, t, :], lg[:, t, :]).then_inc(route_step, 1)
                step(2)
                dve.tensor_tensor(gap[:, :], top[:, :, 0], top[:, :, 1], ALU.subtract)
                for t in range(NT):
                    dve.max_index(topi[:, t, :], top[:, t, :], lg[:, t, :]).then_inc(route_step, 1)
                step(4)
                dve.tensor_copy(topf[:, :, :], topi[:, :, 0:2]).then_inc(route_step, 1)
                step(5)
                dve.tensor_tensor(hot[:, :, :, :].rearrange("p t j e -> p (t j) e"),
                                  iota8[:, :].unsqueeze(1).to_broadcast([P, NT * 2, E]),
                                  topf[:, :, :].rearrange("p t j -> p (t j)").unsqueeze(2).to_broadcast([P, NT * 2, E]),
                                  ALU.is_equal).then_inc(route_step, 2)
                dve.wait_ge(tanh_done, b + 1)
                dve.tensor_scalar(w12[:, :, 0], th[:, :], 0.5, 0.5, ALU.mult, ALU.add)
                dve.tensor_scalar(w12[:, :, 1], th[:, :], -0.5, 0.5, ALU.mult, ALU.add).then_inc(route_step, 1)
                step(8)
                dve.tensor_tensor(hotw[:, :, :, :].rearrange("p t j e -> p (t j) e"),
                                  hot[:, :, :, :].rearrange("p t j e -> p (t j) e"),
                                  w12[:, :, :].rearrange("p t j -> p (t j)").unsqueeze(2).to_broadcast([P, NT * 2, E]),
                                  ALU.mult).then_inc(route_step, 1)
                step(9)
                dve.tensor_tensor(gate[:, r, :, :], hotw[:, :, 0, :], hotw[:, :, 1, :],
                                  ALU.add).then_inc(gate_ready, 1)

            xT(0, 0)
            for c in range(QC):
                qk(0, 0, c)
            route(0, 0)

            def split_h(b, e):
                dve.wait_ge(silu_done, b * E + (e + 1))
                wait_used(dve, e_psum, b * E + max(e - 1, 0))
                dve.tensor_copy(h_hi[:, e % 2, :, :], h_f[:, e % 2, :, :]).then_inc(h_hi_done, 1)
                dve.wait_ge(h_hi_done, b * E + (e + 1))
                dve.tensor_tensor(h_lo[:, e % 2, :, :], h_f[:, e % 2, :, :], h_hi[:, e % 2, :, :].bitcast(F32),
                                  ALU.subtract).then_inc(h_lo_done, 1)

            def add_expert(b, r, e):
                dve.wait_ge(e_psum, b * E + (e + 1))
                if e == 0:
                    dve.wait_ge(residual_ready, b + 1)
                    dve.wait_ge(gate_ready, b + 1)
                else:
                    dve.wait_ge(moe_added, b * E + e)
                for t in range(NT):
                    last = dve.scalar_tensor_tensor(out=acc[:, r, t, :], in0=ps_e[:, t, 0:D],
                                                    scalar=gate[:, r, t, e:e + 1], in1=acc[:, r, t, :],
                                                    op0=ALU.mult, op1=ALU.add)
                last.then_inc(moe_added, 1)

            def batch(b, r, has_next):
                for k in range(PAIRS):
                    if has_next:
                        if k == 0:
                            wait_used(dve, residual_ready, b)
                            wait_used(dve, xT_psum, b)
                            normalise(b + 1, 1 - r)
                        if k == 1:
                            xT(b + 1, 1 - r)
                        if 2 <= k < 2 + QC:
                            qk(b + 1, 1 - r, k - 2)
                        if k == 6:
                            route(b + 1, 1 - r)
                    split_h(b, k)
                    if k >= 1:
                        add_expert(b, r, k - 1)
                dve.wait_ge(pv_done, PAIRS * (b + 1))
                wait_used(dve, yT_psum, b)
                num = ps_num[:, 0:NT * NUMW].rearrange("p (n d) -> p n d", d=HD1)
                dve.tensor_scalar(den[:, :], num[:, :, HD], 2 * EPS_DEN, None, ALU.add).then_inc(den_step, 1)
                dve.wait_ge(den_step, b * 2 + 2)
                dve.reciprocal(rden[:, :], den[:, :]).then_inc(den_step, 1)
                dve.wait_ge(den_step, b * 2 + 3)
                dve.tensor_tensor(y[:, :, :].rearrange("p t (h d) -> p (t h) d", d=HD), num[:, :, 0:HD],
                                  rden[:, :].unsqueeze(2).to_broadcast([P, NT * H, HD]), ALU.mult).then_inc(y_ready, 1)
                add_expert(b, r, E - 1)
                dve.wait_ge(att_psum, b + 1)
                dve.wait_ge(moe_added, E * (b + 1))
                dve.tensor_tensor(acc[:, r, :, :], ps_y[:, 0, :].rearrange("p (t d) -> p t d", d=D),
                                  acc[:, r, :, :], ALU.add).then_inc(out_ready, 1)

            for_batches(dve, batch)

        @block.tensor
        def _(pe):
            def mm3(dst, lhs, rhs):
                pe.matmul(dst, lhs[0], rhs[0], start=True, stop=False)
                pe.matmul(dst, lhs[0], rhs[1], start=False, stop=False)
                return pe.matmul(dst, lhs[1], rhs[0], start=False, stop=True)

            def xT(b, r):
                pe.wait_ge(xn_ready, NT * (b + 1))
                wait_used(pe, lg_read, b)
                for t in range(NT):
                    last = pe.transpose(ps_t[:, t * P:(t + 1) * P], xn[:, r, t, :], ident[:, :])
                last.then_inc(xT_psum, 1)

            def xT_of(r, t=None):
                cols = slice(0, TB) if t is None else slice(t * P, (t + 1) * P)
                return xT_hi[:, r, cols], xT_lo[:, r, cols]

            def v(b, r):
                pe.wait_ge(xT_lo_done, b + 1)
                for t in range(NT):
                    last = mm3(ps_t[:, t * D:(t + 1) * D], xT_of(r, t), (wv_hi[:, :], wv_lo[:, :]))
                last.then_inc(v_psum, 1)

            def qk(b, r, c):
                wait_used(pe, qk_lo_done, b * QC + c)
                for m in range(2):
                    w = [s[:, m, 4 * c:4 * (c + 1), :, :].rearrange("p h c f -> p (h c f)") for s in (wqk_hi, wqk_lo)]
                    last = mm3(ps_qk[:, m, :], w, xT_of(r))
                last.then_inc(qk_psum, 1)

            def r1(b, r):
                pe.wait_ge(v_ready, b + 1)
                mm3(ps_t[:, 0:TB], (rw1_hi[:, :], rw1_lo[:, :]), xT_of(r)).then_inc(r1_psum, 1)

            def logits(b, r):
                pe.wait_ge(r1_ready, b + 1)
                for t in range(NT):
                    pe.matmul(ps_t[:, t * E:(t + 1) * E], r1T[:, r, t * P:(t + 1) * P], rw2_f[:, :],
                              start=True, stop=False)
                    last = pe.matmul(ps_t[:, t * E:(t + 1) * E], ones[0:1, :], rb2_r[:, :], start=False, stop=True)
                last.then_inc(lg_psum, 1)

            def scores(b, r, k):
                wait_used(pe, square_done, b * PAIRS + k)
                for j in range(2):
                    h = 2 * k + j
                    c, rows = h // 4, slice(32 * (h % 4), 32 * (h % 4) + 32)
                    for t, cols in ((0, slice(0, TB)), (1, slice(TB, SW))):
                        dst = ps_s[:, j, cols]
                        q = q_mix[rows, r, c, t * P:TB]
                        keys = slice(t * P, (t + 1) * P)
                        pe.matmul(dst, qk_hi[rows, r, c, 1, keys], q, start=True, stop=False)
                        last = pe.matmul(dst, k_lo[rows, r, c, keys], q, start=False, stop=True)
                last.then_inc(s_psum, 1)

            def hidden(b, r, e):
                wait_used(pe, silu_done, b * E + e)
                for c in range(NC):
                    w = [s[:, e, c * P:(c + 1) * P] for s in (ew1_hi, ew1_lo)]
                    last = mm3(ps_h[:, c, :], w, xT_of(r))
                last.then_inc(h_psum, 1)

            def expert_out(b, e):
                pe.wait_ge(h_lo_done, b * E + (e + 1))
                wait_used(pe, moe_added, b * E + e)
                for t in range(NT):
                    for c in range(NC):
                        h = [s[:, e % 2, c, t * P:(t + 1) * P] for s in (h_hi, h_lo)]
                        w = [s[:, e * NC + c, :] for s in (ew2_hi, ew2_lo)]
                        for n, (a, m) in enumerate(((0, 0), (0, 1), (1, 0))):
                            last = pe.matmul(ps_e[:, t, 0:D], h[a], w[m], start=(c == 0 and n == 0),
                                             stop=(c == NC - 1 and n == 2))
                last.then_inc(e_psum, 1)

            def prefix_v(b, r):
                wait_used(pe, y_ready, b)
                v0, v1 = (v_aug[:, r, t, :, :].rearrange("p h d -> p (h d)") for t in range(NT))
                pe.matmul(ps_num[:, 0:NUMW], causal[:, :], v0, start=True, stop=False, skip_group_check=True)
                pe.matmul(ps_num[:, NUMW:2 * NUMW], ones[:, :], v0, start=False, stop=False, skip_group_check=True)
                pe.matmul(ps_num[:, NUMW:2 * NUMW], causal[:, :], v1, start=False, stop=False, skip_group_check=True)

            def weigh_v(b, r, k):
                pe.wait_ge(mask_done, b * PAIRS + (k + 1))
                for j in range(2):
                    h = 2 * k + j
                    dst = [ps_num[:, t * NUMW + h * HD1:t * NUMW + (h + 1) * HD1] for t in range(NT)]
                    for t, cols, kt in ((0, 0, 0), (1, P, 0), (1, TB, 1)):
                        last = pe.matmul(dst[t], w_att[:, k % 2, j, cols:cols + P], v_aug[:, r, kt, h, :],
                                         start=False, stop=(k == PAIRS - 1 and j == 1), skip_group_check=True)
                last.then_inc(pv_done, 1)

            pe.wait_ge(const_step, CONST_ALL)
            xT(0, 0)
            pe.wait_ge(w_split, W_ATT_SPLIT)
            v(0, 0)
            for c in range(QC):
                qk(0, 0, c)
            r1(0, 0)
            pe.wait_ge(small_in, 16 * 6)
            logits(0, 0)
            pe.wait_ge(ew1_lo_done, E)
            pe.wait_ge(ew2_lo_done, E)

            def batch(b, r, has_next):
                pe.wait_ge(qk_lo_done, QC * (b + 1))
                for k in range(PAIRS):
                    scores(b, r, k)
                    if k == 0:
                        prefix_v(b, r)
                    if has_next:
                        if k == 1:
                            xT(b + 1, 1 - r)
                        if k == 2:
                            v(b + 1, 1 - r)
                        if 2 <= k < 2 + QC:
                            qk(b + 1, 1 - r, k - 2)
                        if k == 5:
                            r1(b + 1, 1 - r)
                        if k == 6:
                            logits(b + 1, 1 - r)
                    hidden(b, r, k)
                    if k >= 1:
                        weigh_v(b, r, k - 1)
                        expert_out(b, k - 1)
                weigh_v(b, r, PAIRS - 1)
                expert_out(b, E - 1)
                pe.wait_ge(y_ready, b + 1)
                wait_used(pe, out_ready, b)
                for t in range(NT):
                    pe.transpose(ps_y[:, 0, t * P:(t + 1) * P], y[:, t, :], ident[:, :])
                    last = pe.transpose(ps_y[0:E, 1, t * P:(t + 1) * P], gate[:, r, t, :], ident[:, :])
                last.then_inc(yT_psum, 1)
                pe.wait_ge(yT_ready, b + 1)
                for t in range(NT):
                    pe.matmul(ps_y[:, 0, t * D:(t + 1) * D], yT[:, t * P:(t + 1) * P], wo_f[:, :],
                              start=True, stop=False)
                    last = pe.matmul(ps_y[:, 0, t * D:(t + 1) * D], gateT[:, t * P:(t + 1) * P], eb2_r[:, :],
                                     start=False, stop=True)
                last.then_inc(att_psum, 1)

            for_batches(pe, batch)


def kernel(**inputs):
    import numpy as np
    import concourse.bacc as bacc
    from concourse.bass_utils import run_bass_kernel_spmd

    g = {k: np.asarray(v) for k, v in inputs.items()}
    A, M = "L0_attn_", "L0_ffn_"
    E, _, HID = g[M + "ew1"].shape
    laid = {
        "x": g[A + "hidden_states"],
        "wqT": g[A + "Wq"].T, "wkT": g[A + "Wk"].T, "wvT": g[A + "Wv"].T, "woT": g[A + "Wo"].T,
        "rw1": g[M + "rw1"], "rb1": g[M + "rb1"].reshape(-1, 1),
        "rw2": g[M + "rw2"], "rb2": g[M + "rb2"].reshape(1, -1),
        "ew1": g[M + "ew1"],
        "eb1": g[M + "eb1"].reshape(E * (HID // P), P).T,
        "ew2": g[M + "ew2"], "eb2": g[M + "eb2"],
    }
    nc = bacc.Bacc("TRN2", target_bir_lowering=False, num_devices=1)
    arrays, args = {}, []
    for name, a in laid.items():
        arrays[name] = np.ascontiguousarray(a)
        args.append(nc.dram_tensor(name, a.shape, mybir.dt.from_np(a.dtype), kind="ExternalInput").ap())
    args.append(nc.dram_tensor("out", laid["x"].shape, F32, kind="ExternalOutput").ap())
    fused_layer(nc, *args)
    r = run_bass_kernel_spmd(nc, [arrays], core_ids=[0])
    return r.results[0]["out"]
```

```python
from contextlib import ExitStack

import concourse.bass as bass
from concourse import mybir

F32 = mybir.dt.float32
F32R = mybir.dt.float32r
BF16 = mybir.dt.bfloat16
I32 = mybir.dt.int32
U32 = mybir.dt.uint32
ALU = mybir.AluOpType
ACT = mybir.ActivationFunctionType

P = 128
RD = 4.0
EPS_LN = 1e-5
EPS_DEN = 1e-12


def fused_layer(nc, x, wqT, wkT, wvT, woT, rw1, rb1, rw2, rb2, ew1, eb1, ew2, eb2, out):
    B, TB, D = x.shape
    NT = TB // P
    TILES = B * NT
    FD = 16
    H = wqT.shape[1] // FD
    HD = D // H
    HD1 = HD + 1
    E, _, HID = ew1.shape
    NC = HID // P
    PAIRS = H // 2
    NG = H * FD // P
    Q_SLOTS = (0, 1, 2, 0, 1, 0)
    K_SLOTS = (0, 0, 0, 1, 1, 2)
    KS = FD * len(Q_SLOTS)
    STACK_DMAS = 2 * len(Q_SLOTS)
    SW = TB + P
    VG = 32
    VROWS = NT * 4
    assert D == P and NT == 2 and PAIRS == E and NC == 2 and NG == 2

    x_v = x.rearrange("b (t p) d -> p (b t) d", p=P)
    out_v = out.rearrange("b (t p) d -> p (b t) d", p=P)
    parts_d = nc.dram_tensor("parts_scratch", (2, 2 * 3, H * FD, TB), BF16, kind="Internal").ap()
    gate_d = nc.dram_tensor("gate_scratch", (2, E, TB), F32, kind="Internal").ap()

    with ExitStack() as ctx:
        def sb(name, shape, dt=F32):
            return ctx.enter_context(nc.sbuf_tensor(name, shape, dt))

        def bank(name, shape):
            return ctx.enter_context(nc.psum_tensor(name, shape, F32))

        def sem(name):
            return ctx.enter_context(nc.semaphore(name))

        ident = sb("ident", [P, P])
        before = sb("before", [P, TB])
        ones = sb("ones", [1, P])
        iota8 = sb("iota8", [P, E])
        den_row = sb("den_row", [P, 8, VG])
        wq_f = sb("wq_f", [P, H * FD])
        wk_f = sb("wk_f", [P, H * FD])
        wv_f = sb("wv_f", [P, D])
        wo_f = sb("wo_f", [P, D])
        rw1_f = sb("rw1_f", [P, D])
        rw2_f = sb("rw2_f", [P, E])
        rb1_c = sb("rb1_c", [P, 1])
        rb2_r = sb("rb2_r", [1, E])
        eb1_c = sb("eb1_c", [P, E * NC])
        eb2_c = sb("eb2_c", [P, E])
        ew1_f = sb("ew1_f", [P, E, HID])
        ew2_f = sb("ew2_f", [P, E * NC, D])
        wqk_hi = sb("wqk_hi", [P, 2, H * FD], F32R)
        wqk_lo = sb("wqk_lo", [P, 2, H * FD], F32R)
        wv_hi = sb("wv_hi", [P, 8, VG], F32R)
        wv_lo = sb("wv_lo", [P, 8, VG], F32R)
        rw1_hi = sb("rw1_hi", [P, D], F32R)
        rw1_lo = sb("rw1_lo", [P, D], F32R)
        ew1_hi = sb("ew1_hi", [P, E, HID], F32R)
        ew1_lo = sb("ew1_lo", [P, E, HID], F32R)
        ew2_hi = sb("ew2_hi", [P, E * NC, D], F32R)
        ew2_lo = sb("ew2_lo", [P, E * NC, D], F32R)

        x_all = sb("x_all", [P, TILES, D])
        stats = sb("stats", [P, TILES, 6])
        mv = sb("mv", [P, TILES, 2])
        var_eps = sb("var_eps", [P, TILES])
        inv_var = sb("inv_var", [P, TILES])
        rstd0 = sb("rstd0", [P, TILES])
        newton = sb("newton", [P, TILES])
        rstd = sb("rstd", [P, TILES])
        xn = sb("xn", [P, 2, NT, D])
        xT_hi = sb("xT_hi", [P, 2, TB], F32R)
        xT_lo = sb("xT_lo", [P, 2, TB], F32R)
        q_stack = sb("q_stack", [KS, 2, H, TB], BF16)
        k_stack = sb("k_stack", [KS, 2, H, TB], BF16)
        v_pad = sb("v_pad", [P, 2, NT, 8, VG])
        v_b = sb("v_b", [P, 2, NT, 8, 2 * HD1])
        r1T = sb("r1T", [P, 2, TB])
        gate = sb("gate", [P, 2, NT, E])
        oT = sb("oT", [P, 2, TB])
        gate_b = sb("gate_b", [P, 2, E, TB])
        parts = sb("parts", [P, NG, 2, 3, TB], BF16)
        rest = sb("rest", [P, NG, 2, TB])
        gateT = sb("gateT", [E, TB])
        w_att = sb("w_att", [P, PAIRS, 2, SW])
        yn = sb("yn", [P, 2, TB])
        y = sb("y", [P, NT, D])
        yT = sb("yT", [P, TB])
        h_f = sb("h_f", [P, 2, NC, TB])
        weighed = sb("weighed", [P, 2, TB])
        h_hi = sb("h_hi", [P, 2, NC, TB], F32R)
        h_lo = sb("h_lo", [P, 2, NC, TB], F32R)
        lg = sb("lg", [P, NT, E])
        top = sb("top", [P, NT, 8])
        topi = sb("topi", [P, NT, 8], U32)
        topf = sb("topf", [P, NT, 2])
        gap = sb("gap", [P, NT])
        th = sb("th", [P, NT])
        w12 = sb("w12", [P, NT, 2])
        hot = sb("hot", [P, NT, 2, E])
        hotw = sb("hotw", [P, NT, 2, E])
        den = sb("den", [P, VROWS * 2, 2])
        rden = sb("rden", [P, VROWS * 2, 2])

        ps_s = bank("ps_s", [P, 2, 512])
        ps_h = bank("ps_h", [P, 2, 512])
        ps_o = bank("ps_o", [P, 512])
        ps_y = bank("ps_y", [P, 2, TB])
        ps_t = bank("ps_t", [P, 512])
        ps_q = bank("ps_q", [P, 2, TB])

        x_in = [sem(f"x_in{g}") for g in range(4)]
        wqkvr_in = sem("wqkvr_in")
        small_in = sem("small_in")
        ew1_in = sem("ew1_in")
        ew2_in = sem("ew2_in")
        const_step = sem("const_step")
        w_split = sem("w_split")
        ew1_hi_done = sem("ew1_hi_done")
        ew1_lo_done = sem("ew1_lo_done")
        ew2_hi_done = sem("ew2_hi_done")
        ew2_lo_done = sem("ew2_lo_done")
        ln_step = sem("ln_step")
        sqrt_done = sem("sqrt_done")
        xn_ready = sem("xn_ready")
        residual_ready = sem("residual_ready")
        xT_psum = sem("xT_psum")
        xT_hi_done = sem("xT_hi_done")
        xT_lo_done = sem("xT_lo_done")
        r1_psum = sem("r1_psum")
        r1_ready = sem("r1_ready")
        lg_psum = sem("lg_psum")
        lg_read = sem("lg_read")
        route_step = sem("route_step")
        tanh_done = sem("tanh_done")
        gate_ready = sem("gate_ready")
        gateT_psum = sem("gateT_psum")
        gateT_ready = sem("gateT_ready")
        gate_stored = sem("gate_stored")
        gate_in = sem("gate_in")
        v_psum = sem("v_psum")
        v_ready = sem("v_ready")
        q_psum = sem("q_psum")
        part_h_done = sem("part_h_done")
        rest_done = sem("rest_done")
        part_m_done = sem("part_m_done")
        parts_ready = sem("parts_ready")
        parts_stored = sem("parts_stored")
        stack_in = sem("stack_in")
        s_psum = sem("s_psum")
        square_done = sem("square_done")
        mask_done = sem("mask_done")
        pv_done = sem("pv_done")
        h_psum = sem("h_psum")
        silu_done = sem("silu_done")
        h_hi_done = sem("h_hi_done")
        h_lo_done = sem("h_lo_done")
        o_psum = sem("o_psum")
        o_weighed = sem("o_weighed")
        o_added = sem("o_added")
        yn_ready = sem("yn_ready")
        num_psum = sem("num_psum")
        den_step = sem("den_step")
        y_ready = sem("y_ready")
        out_psum = sem("out_psum")
        moe_added = sem("moe_added")
        yT_psum = sem("yT_psum")
        yT_ready = sem("yT_ready")
        att_psum = sem("att_psum")
        out_ready = sem("out_ready")
        out_stored = sem("out_stored")

        ROUTE_STEPS = 9
        HALF = PAIRS // 2
        SMALL_DMAS = 6

        def for_batches(eng, batch):
            batch(0, 0, False, True)
            with eng.Fori(0, B // 2 - 1) as i:
                batch(i * 2 + 1, 1, True, True)
                batch(i * 2 + 2, 0, True, True)
            batch(B - 1, 1, True, False)

        def wait_used(eng, what, n):
            if not isinstance(n, int) or n > 0:
                eng.wait_ge(what, n)

        block = ctx.enter_context(nc.Block())

        @block.sync
        def _(sp):
            for g in range(4):
                n = TILES // 4
                sp.dma_start(x_all[:, g * n:(g + 1) * n, :], x_v[:, g * n:(g + 1) * n, :]).then_inc(x_in[g], 16)
            sp.dma_start(ew1_f[:, :, :], ew1.rearrange("e d h -> d e h")).then_inc(ew1_in, 16)
            sp.dma_start(ew2_f[:, :, :], ew2.rearrange("e (c p) d -> p (e c) d", p=P)).then_inc(ew2_in, 16)

            def store_parts(b, r):
                wait_used(sp, stack_in, b * (16 * STACK_DMAS))
                for g in range(NG):
                    sp.nop(nofuse=True)
                    sp.wait_ge(parts_ready, b * NG + (g + 1))
                    sp.nop(nofuse=True)
                    sp.dma_start(parts_d[r, :, g * P:(g + 1) * P, :].rearrange("n p t -> p n t"),
                                 parts[:, g, :, :, :].rearrange("p m s t -> p (m s) t")).then_inc(parts_stored, 16)

            def load_stacks(b, r, used):
                sp.wait_ge(parts_stored, (b + 1) * (16 * NG))
                sp.nop(nofuse=True)
                wait_used(sp, s_psum, used)
                sp.nop(nofuse=True)
                for stack, m, slots in ((q_stack, 0, Q_SLOTS), (k_stack, 1, K_SLOTS)):
                    for n, part in enumerate(slots):
                        sp.dma_start(stack[n * FD:(n + 1) * FD, r, :, :],
                                     parts_d[r, 3 * m + part, :, :].rearrange("(h f) t -> f h t", f=FD)
                                     ).then_inc(stack_in, 16)

            def spread_gate(b, r, used):
                sp.wait_ge(gateT_ready, b + 1)
                sp.nop(nofuse=True)
                wait_used(sp, gate_in, b * 16)
                sp.nop(nofuse=True)
                sp.dma_start(gate_d[r, :, :], gateT[:, :]).then_inc(gate_stored, 16)
                sp.wait_ge(gate_stored, (b + 1) * 16)
                sp.nop(nofuse=True)
                wait_used(sp, o_weighed, used)
                sp.nop(nofuse=True)
                sp.dma_start(gate_b[:, r, :, :].rearrange("p e t -> p (e t)"),
                             gate_d[r:r + 1, :, :].rearrange("o e t -> o (e t)").to_broadcast([P, E * TB])
                             ).then_inc(gate_in, 16)

            def store(b):
                sp.wait_ge(out_ready, b + 1)
                sp.nop(nofuse=True)
                sp.dma_start(out_v[:, bass.ds(b * NT, NT), :], x_all[:, bass.ds(b * NT, NT), :]).then_inc(out_stored, 16)

            store_parts(0, 0)
            load_stacks(0, 0, 0)
            spread_gate(0, 0, 0)

            def batch(b, r, has_last, has_next):
                if has_next:
                    store_parts(b + 1, 1 - r)
                    load_stacks(b + 1, 1 - r, b * PAIRS)
                    spread_gate(b + 1, 1 - r, b * E)
                if has_last:
                    store(b - 1)

            for_batches(sp, batch)
            store(B - 1)
            sp.wait_ge(out_stored, 16 * B)

        @block.gpsimd
        def _(pool):
            pool.memset(ident[:, :], 0.0).then_inc(const_step, 1)
            pool.memset(before[:, :], 1.0).then_inc(const_step, 1)
            pool.memset(ones[:, :], 1.0).then_inc(const_step, 1)
            pool.memset(den_row[:, :, :], 0.0).then_inc(const_step, 1)
            pool.wait_ge(const_step, 4)
            pool.affine_select(out=ident[:, :], in_=ident[:, :], compare_op=ALU.not_equal, fill=1.0,
                               base=0, pattern=[[-1, P]], channel_multiplier=1).then_inc(const_step, 1)
            pool.affine_select(out=before[:, 0:P], in_=before[:, 0:P], compare_op=ALU.is_ge, fill=0.0,
                               base=0, pattern=[[1, P]], channel_multiplier=-1).then_inc(const_step, 1)
            pool.memset(den_row[:, :, HD:2 * HD1:HD1], 1.0).then_inc(const_step, 1)
            for w in (wv_hi, wv_lo):
                pool.memset(w[:, :, :].bitcast(F32), 0.0).then_inc(const_step, 1)
            pool.memset(v_b[:, :, :, :, :], 0.0).then_inc(const_step, 1)
            pool.iota(iota8[:, :], pattern=[[1, E]], base=0, channel_multiplier=0,
                      allow_small_or_imprecise_dtypes=True).then_inc(const_step, 1)

            def residual(b, r):
                pool.wait_ge(xn_ready, NT * (b + 1))
                pool.tensor_tensor(x_all[:, bass.ds(b * NT, NT), :], x_all[:, bass.ds(b * NT, NT), :],
                                   xn[:, r, :, :], ALU.add).then_inc(residual_ready, 1)

            def part_l(b, g):
                pool.wait_ge(part_m_done, b * NG + (g + 1))
                pool.tensor_tensor(parts[:, g, :, 2, :], rest[:, g, :, :], parts[:, g, :, 1, :],
                                   ALU.subtract).then_inc(parts_ready, 1)

            def low_weights(e):
                pool.wait_ge(ew1_hi_done, e + 1)
                pool.tensor_tensor(ew1_lo[:, e, :], ew1_f[:, e, :], ew1_hi[:, e, :].bitcast(F32),
                                   ALU.subtract).then_inc(ew1_lo_done, 1)
                pool.wait_ge(ew2_hi_done, e + 1)
                pool.tensor_tensor(ew2_lo[:, NC * e:NC * (e + 1), :], ew2_f[:, NC * e:NC * (e + 1), :],
                                   ew2_hi[:, NC * e:NC * (e + 1), :].bitcast(F32),
                                   ALU.subtract).then_inc(ew2_lo_done, 1)

            def mask(b, k):
                pool.wait_ge(square_done, b * PAIRS + (k + 1))
                pool.nop(nofuse=True)
                for j in range(2):
                    diag = w_att[:, k, j, :].rearrange("p (n q) -> p n q", q=P)[:, 0:3:2, :]
                    last = pool.affine_select(out=diag, in_=diag, compare_op=ALU.is_ge, fill=0.0, base=0,
                                              pattern=[[0, 2], [1, P]], channel_multiplier=-1)
                last.then_inc(mask_done, 1)

            def add_expert(b, r, e):
                pool.wait_ge(o_weighed, b * E + (e + 1))
                if e > 1:
                    pool.wait_ge(o_added, b * (E - 1) + (e - 1))
                pool.tensor_tensor(oT[:, r, :], oT[:, r, :], weighed[:, e % 2, :], ALU.add).then_inc(o_added, 1)

            for g in range(NG):
                part_l(0, g)
            low_weights(0)
            low_weights(1)

            def batch(b, r, has_last, has_next):
                for k in range(PAIRS):
                    mask(b, k)
                    if k >= 3:
                        add_expert(b, r, k - 2)
                    elif has_last and k < 2:
                        add_expert(b - 1, 1 - r, E - 2 + k)
                    if has_next and k in (2, 3):
                        part_l(b + 1, k - 2)
                    if k == 5:
                        residual(b, r)
                    if not has_last and k + 2 < E:
                        low_weights(k + 2)

            for_batches(pool, batch)
            add_expert(B - 1, 1, E - 2)
            add_expert(B - 1, 1, E - 1)

        @block.scalar
        def _(act):
            for dst, src in ((wq_f, wqT), (wk_f, wkT), (wv_f, wvT), (rw1_f, rw1)):
                act.dma_start(dst[:, :], src).then_inc(wqkvr_in, 16)
            for dst, src in ((rb1_c, rb1), (rw2_f, rw2), (rb2_r, rb2), (eb1_c, eb1), (wo_f, woT), (eb2_c, eb2)):
                act.dma_start(dst[:, :], src).then_inc(small_in, 16)
            act.wait_ge(ln_step, 3)
            act.activation(rstd0[:, :], inv_var[:, :], ACT.Sqrt).then_inc(sqrt_done, 1)

            def split_hi(e):
                act.activation(ew1_hi[:, e, :], ew1_f[:, e, :], ACT.Copy).then_inc(ew1_hi_done, 1)
                act.activation(ew2_hi[:, NC * e:NC * (e + 1), :], ew2_f[:, NC * e:NC * (e + 1), :],
                               ACT.Copy).then_inc(ew2_hi_done, 1)

            def xT(b, r):
                act.wait_ge(xT_psum, b + 1)
                act.activation(xT_hi[:, r, :], ps_t[:, 0:TB], ACT.Copy).then_inc(xT_hi_done, 1)

            def part_h(b, g):
                act.wait_ge(q_psum, b * NG + (g + 1))
                if g == 0:
                    wait_used(act, parts_stored, b * (16 * NG))
                act.activation(parts[:, g, :, 0, :], ps_q[:, :, :], ACT.Copy).then_inc(part_h_done, 1)

            def part_m(b, g):
                act.wait_ge(rest_done, b * NG + (g + 1))
                act.activation(parts[:, g, :, 1, :], rest[:, g, :, :], ACT.Copy).then_inc(part_m_done, 1)

            def r1(b, r):
                act.wait_ge(r1_psum, b + 1)
                act.activation(r1T[:, r, :], ps_t[:, 0:TB], ACT.Silu, bias=rb1_c[:, 0:1]).then_inc(r1_ready, 1)

            def tanh(b):
                act.wait_ge(route_step, b * ROUTE_STEPS + 7)
                act.activation(th[:, :], gap[:, :], ACT.Tanh, scale=0.5).then_inc(tanh_done, 1)

            def gate_T(b):
                act.wait_ge(gateT_psum, b + 1)
                wait_used(act, gate_stored, b * 16)
                act.activation(gateT[:, :], ps_t[0:E, 0:TB], ACT.Copy).then_inc(gateT_ready, 1)

            act.wait_ge(small_in, 16 * SMALL_DMAS)
            xT(0, 0)
            r1(0, 0)
            for g in range(NG):
                part_h(0, g)
                part_m(0, g)
            tanh(0)
            act.wait_ge(ew1_in, 16)
            act.wait_ge(ew2_in, 16)
            split_hi(0)
            gate_T(0)
            for e in range(1, E):
                split_hi(e)

            def square(b, k):
                act.wait_ge(s_psum, b * PAIRS + (k + 1))
                if k % HALF == 0:
                    wait_used(act, pv_done, b * 2 - 1 + k // HALF)
                act.activation(w_att[:, k, :, :], ps_s[:, :, 0:SW], ACT.Square, bias=1.0,
                               scale=1.0 / RD).then_inc(square_done, 1)

            def silu(b, e):
                act.wait_ge(h_psum, b * E + (e + 1))
                wait_used(act, h_lo_done, b * E + max(e - 1, 0))
                for c in range(NC):
                    last = act.activation(h_f[:, e % 2, c, :], ps_h[:, e % 2, c * TB:(c + 1) * TB], ACT.Silu,
                                          bias=eb1_c[:, e * NC + c:e * NC + c + 1])
                last.then_inc(silu_done, 1)

            def leave(b):
                act.wait_ge(pv_done, b * 2 + 2)
                wait_used(act, num_psum, b)
                act.activation(yn[:, :, :], ps_y[:, :, :], ACT.Copy).then_inc(yn_ready, 1)

            def y_T(b):
                act.wait_ge(yT_psum, b + 1)
                wait_used(act, att_psum, b)
                act.activation(yT[:, :], ps_q[:, 0, :], ACT.Copy).then_inc(yT_ready, 1)

            def batch(b, r, has_last, has_next):
                for k in range(PAIRS):
                    square(b, k)
                    silu(b, k)
                    if has_next:
                        if k == 0:
                            xT(b + 1, 1 - r)
                        if k == 1:
                            r1(b + 1, 1 - r)
                        if k in (1, 2):
                            part_h(b + 1, k - 1)
                        if k in (2, 3):
                            part_m(b + 1, k - 2)
                        if k == 3:
                            tanh(b + 1)
                        if k == 5:
                            gate_T(b + 1)
                    if has_last:
                        if k == 1:
                            leave(b - 1)
                        if k == 5:
                            y_T(b - 1)

            for_batches(act, batch)
            leave(B - 1)
            y_T(B - 1)

        @block.vector
        def _(dve):
            for g in range(4):
                dve.wait_ge(x_in[g], 16)
                for t in range(g * TILES // 4, (g + 1) * TILES // 4):
                    last = dve.bn_stats(stats[:, t, :], x_all[:, t, :])
            last.then_inc(ln_step, 1)
            dve.wait_ge(ln_step, 1)
            for t in range(TILES):
                last = dve.bn_aggr(mv[:, t, :], stats[:, t, :])
            last.then_inc(den_step, 1)
            dve.wait_ge(den_step, 1)
            dve.tensor_scalar(var_eps[:, :], mv[:, :, 1], EPS_LN, None, ALU.add).then_inc(ln_step, 1)
            dve.wait_ge(ln_step, 2)
            dve.reciprocal(inv_var[:, :], var_eps[:, :]).then_inc(ln_step, 1)
            dve.wait_ge(sqrt_done, 1)
            dve.tensor_tensor(newton[:, :], rstd0[:, :], rstd0[:, :], ALU.mult).then_inc(ln_step, 1)
            dve.wait_ge(ln_step, 4)
            dve.tensor_tensor(newton[:, :], newton[:, :], var_eps[:, :], ALU.mult).then_inc(ln_step, 1)
            dve.wait_ge(ln_step, 5)
            dve.tensor_scalar(newton[:, :], newton[:, :], -0.5, 1.5, ALU.mult, ALU.add).then_inc(ln_step, 1)
            dve.wait_ge(ln_step, 6)
            dve.tensor_tensor(rstd[:, :], rstd0[:, :], newton[:, :], ALU.mult).then_inc(ln_step, 1)
            dve.wait_ge(ln_step, 7)

            def normalise(b, r):
                for t in range(NT):
                    dve.tensor_scalar(xn[:, r, t, :], x_all[:, bass.ds(b * NT + t, 1), :].squeeze(1),
                                      mv[:, bass.ds(b * NT + t, 1), 0:1].squeeze(1),
                                      rstd[:, bass.ds(b * NT + t, 1)],
                                      ALU.subtract, ALU.mult).then_inc(xn_ready, 1)

            normalise(0, 0)
            dve.wait_ge(wqkvr_in, 16 * 4)
            dve.wait_ge(const_step, 9)
            pairs = [(wqk_hi[:, 0, :], wqk_lo[:, 0, :], wq_f[:, :]), (wqk_hi[:, 1, :], wqk_lo[:, 1, :], wk_f[:, :]),
                     (rw1_hi[:, :], rw1_lo[:, :], rw1_f[:, :])]
            wv_pairs = wv_f[:, :].rearrange("p (g i d) -> p g i d", i=2, d=HD)
            pairs += [(wv_hi[:, :, i * HD1:i * HD1 + HD], wv_lo[:, :, i * HD1:i * HD1 + HD], wv_pairs[:, :, i, :])
                      for i in range(2)]
            for hi, lo, w in pairs:
                dve.tensor_copy(hi, w).then_inc(w_split, 1)
            dve.wait_ge(w_split, len(pairs))
            for hi, lo, w in pairs:
                dve.tensor_tensor(lo, w, hi.bitcast(F32), ALU.subtract).then_inc(w_split, 1)

            def xT(b, r):
                dve.wait_ge(xT_hi_done, b + 1)
                dve.tensor_tensor(xT_lo[:, r, :], ps_t[:, 0:TB], xT_hi[:, r, :].bitcast(F32),
                                  ALU.subtract).then_inc(xT_lo_done, 1)

            def qk_rest(b, g):
                dve.wait_ge(part_h_done, b * NG + (g + 1))
                wait_used(dve, parts_ready, (b - 1) * NG + (g + 1))
                dve.tensor_tensor(rest[:, g, :, :], ps_q[:, :, :], parts[:, g, :, 0, :],
                                  ALU.subtract).then_inc(rest_done, 1)

            def route_choose(b):
                def step(n):
                    dve.wait_ge(route_step, b * ROUTE_STEPS + n)

                dve.wait_ge(lg_psum, b + 1)
                dve.tensor_copy(lg[:, :, :].rearrange("p t e -> p (t e)"), ps_t[:, 0:NT * E]).then_inc(lg_read, 1)
                dve.wait_ge(lg_read, b + 1)
                dve.nop(nofuse=True)
                for t in range(NT):
                    dve.max(top[:, t, :], lg[:, t, :]).then_inc(route_step, 1)
                step(2)
                dve.tensor_tensor(gap[:, :], top[:, :, 0], top[:, :, 1], ALU.subtract)
                for t in range(NT):
                    dve.max_index(topi[:, t, :], top[:, t, :], lg[:, t, :]).then_inc(route_step, 1)
                step(4)
                dve.tensor_copy(topf[:, :, :], topi[:, :, 0:2]).then_inc(route_step, 1)
                step(5)
                dve.tensor_tensor(hot[:, :, :, :].rearrange("p t j e -> p (t j) e"),
                                  iota8[:, :].unsqueeze(1).to_broadcast([P, NT * 2, E]),
                                  topf[:, :, :].rearrange("p t j -> p (t j)").unsqueeze(2).to_broadcast([P, NT * 2, E]),
                                  ALU.is_equal).then_inc(route_step, 2)

            def route_weigh(b, r):
                dve.wait_ge(tanh_done, b + 1)
                dve.tensor_scalar(w12[:, :, 0], th[:, :], 0.5, 0.5, ALU.mult, ALU.add)
                dve.tensor_scalar(w12[:, :, 1], th[:, :], -0.5, 0.5, ALU.mult, ALU.add).then_inc(route_step, 1)
                dve.wait_ge(route_step, b * ROUTE_STEPS + 8)
                dve.tensor_tensor(hotw[:, :, :, :].rearrange("p t j e -> p (t j) e"),
                                  hot[:, :, :, :].rearrange("p t j e -> p (t j) e"),
                                  w12[:, :, :].rearrange("p t j -> p (t j)").unsqueeze(2).to_broadcast([P, NT * 2, E]),
                                  ALU.mult).then_inc(route_step, 1)
                dve.wait_ge(route_step, b * ROUTE_STEPS + 9)
                dve.tensor_tensor(gate[:, r, :, :], hotw[:, :, 0, :], hotw[:, :, 1, :],
                                  ALU.add).then_inc(gate_ready, 1)

            def v(b, r):
                dve.wait_ge(v_psum, b + 1)
                dve.tensor_tensor(v_b[:, r, :, :, HD1:2 * HD1].rearrange("p t g d -> p (t g) d"),
                                  ps_t[:, :].rearrange("p (n c) -> p n c", c=VG)[:, :, HD1:2 * HD1],
                                  den_row[:, 0:1, HD1:2 * HD1].to_broadcast([P, NT * 8, HD1]), ALU.add)
                dve.tensor_tensor(v_pad[:, r, :, :, :].rearrange("p t g c -> p t (g c)"),
                                  ps_t[:, :].rearrange("p (t c) -> p t c", t=NT),
                                  den_row[:, :, :].rearrange("p g c -> p (g c)").unsqueeze(1).to_broadcast([P, NT, 8 * VG]),
                                  ALU.add).then_inc(v_ready, 1)

            xT(0, 0)
            dve.wait_ge(const_step, 11)
            for g in range(NG):
                qk_rest(0, g)
            route_choose(0)
            route_weigh(0, 0)
            v(0, 0)

            def split_h(b, e):
                dve.wait_ge(silu_done, b * E + (e + 1))
                wait_used(dve, o_psum, b * E + max(e - 1, 0))
                dve.tensor_copy(h_hi[:, e % 2, :, :], h_f[:, e % 2, :, :]).then_inc(h_hi_done, 1)
                dve.wait_ge(h_hi_done, b * E + (e + 1))
                dve.tensor_tensor(h_lo[:, e % 2, :, :], h_f[:, e % 2, :, :], h_hi[:, e % 2, :, :].bitcast(F32),
                                  ALU.subtract).then_inc(h_lo_done, 1)

            def weigh(b, r, e):
                if e == 0:
                    dve.wait_ge(gate_in, (b + 1) * 16)
                    dst = oT[:, r, :]
                else:
                    dst = weighed[:, e % 2, :]
                    if e > 2:
                        dve.wait_ge(o_added, b * (E - 1) + (e - 2))
                    else:
                        wait_used(dve, o_added, b * (E - 1))
                dve.wait_ge(o_psum, b * E + (e + 1))
                dve.scalar_tensor_tensor(out=dst, in0=ps_o[:, 0:TB], scalar=eb2_c[:, e:e + 1],
                                         in1=gate_b[:, r, e, :], op0=ALU.add, op1=ALU.mult).then_inc(o_weighed, 1)

            def divide(b):
                dve.wait_ge(num_psum, b + 1)
                num = ps_q[:, :, :].rearrange("p t (g c) -> p (t g) c", c=VG)[:, :, 0:2 * HD1].rearrange(
                    "p g (i d) -> p g i d", d=HD1)
                dve.tensor_scalar(den[:, :, :], num[:, :, :, HD], 2 * EPS_DEN, None, ALU.add).then_inc(den_step, 1)
                dve.wait_ge(den_step, b * 2 + 2)
                dve.reciprocal(rden[:, :, :], den[:, :, :]).then_inc(den_step, 1)
                dve.wait_ge(den_step, b * 2 + 3)
                dve.tensor_tensor(y[:, :, :].rearrange("p t (g i d) -> p (t g) i d", i=2, d=HD), num[:, :, :, 0:HD],
                                  rden[:, :, :].unsqueeze(3).to_broadcast([P, VROWS * 2, 2, HD]),
                                  ALU.mult).then_inc(y_ready, 1)

            def add_experts(b):
                dve.wait_ge(out_psum, b + 1)
                dve.wait_ge(residual_ready, b + 1)
                res = x_all[:, bass.ds(b * NT, NT), :]
                dve.tensor_tensor(res, ps_t[:, 0:TB].rearrange("p (t d) -> p t d", d=D), res, ALU.add).then_inc(moe_added, 1)

            def add_attention(b):
                dve.wait_ge(att_psum, b + 1)
                dve.wait_ge(moe_added, b + 1)
                res = x_all[:, bass.ds(b * NT, NT), :]
                dve.tensor_tensor(res, ps_q[:, 0, :].rearrange("p (t d) -> p t d", d=D), res, ALU.add).then_inc(out_ready, 1)

            def batch(b, r, has_last, has_next):
                for k in range(PAIRS):
                    if has_next and k == 0:
                        wait_used(dve, residual_ready, b)
                        wait_used(dve, xT_psum, b)
                        normalise(b + 1, 1 - r)
                    if k > 0:
                        split_h(b, k - 1)
                    elif has_last:
                        split_h(b - 1, E - 1)
                    if k > 1:
                        weigh(b, r, k - 2)
                    elif has_last:
                        weigh(b - 1, 1 - r, E - 2 + k)
                    if has_next:
                        if k == 0:
                            xT(b + 1, 1 - r)
                        if k in (1, 2):
                            qk_rest(b + 1, k - 1)
                        if k == 3:
                            route_choose(b + 1)
                        if k == 4:
                            route_weigh(b + 1, 1 - r)
                            v(b + 1, 1 - r)
                    if has_last:
                        if k == 4:
                            divide(b - 1)
                        if k == 7:
                            add_experts(b - 1)
                            add_attention(b - 1)

            for_batches(dve, batch)
            split_h(B - 1, E - 1)
            weigh(B - 1, 1, E - 2)
            divide(B - 1)
            weigh(B - 1, 1, E - 1)
            add_experts(B - 1)
            add_attention(B - 1)

        @block.tensor
        def _(pe):
            def mm3(dst, lhs, rhs, start=True, stop=True, **kw):
                pe.matmul(dst, lhs[0], rhs[0], start=start, stop=False, **kw)
                pe.matmul(dst, lhs[0], rhs[1], start=False, stop=False, **kw)
                return pe.matmul(dst, lhs[1], rhs[0], start=False, stop=stop, **kw)

            def xT_of(r, cols=slice(0, TB)):
                return xT_hi[:, r, cols], xT_lo[:, r, cols]

            def xT(b, r):
                pe.wait_ge(xn_ready, NT * (b + 1))
                wait_used(pe, gateT_ready, b)
                for t in range(NT):
                    last = pe.transpose(ps_t[:, t * P:(t + 1) * P], xn[:, r, t, :], ident[:, :])
                last.then_inc(xT_psum, 1)

            def r1(b, r):
                pe.wait_ge(xT_lo_done, b + 1)
                mm3(ps_t[:, 0:TB], (rw1_hi[:, :], rw1_lo[:, :]), xT_of(r)).then_inc(r1_psum, 1)

            def logits(b, r):
                pe.wait_ge(r1_ready, b + 1)
                for t in range(NT):
                    pe.matmul(ps_t[:, t * E:(t + 1) * E], r1T[:, r, t * P:(t + 1) * P], rw2_f[:, :],
                              start=True, stop=False)
                    last = pe.matmul(ps_t[:, t * E:(t + 1) * E], ones[0:1, :], rb2_r[:, :], start=False, stop=True)
                last.then_inc(lg_psum, 1)

            def v(b, r):
                pe.wait_ge(lg_read, b + 1)
                w = [s[:, :, :].rearrange("p g c -> p (g c)") for s in (wv_hi, wv_lo)]
                for t in range(NT):
                    last = mm3(ps_t[:, t * TB:(t + 1) * TB], xT_of(r, slice(t * P, (t + 1) * P)), w)
                last.then_inc(v_psum, 1)

            def gate_T(b, r):
                pe.wait_ge(v_ready, b + 1)
                pe.wait_ge(gate_ready, b + 1)
                for t in range(NT):
                    last = pe.transpose(ps_t[0:E, t * P:(t + 1) * P], gate[:, r, t, :], ident[:, :])
                last.then_inc(gateT_psum, 1)

            def qk(b, r, g):
                if g > 0:
                    pe.wait_ge(rest_done, b * NG + g)
                for m in range(2):
                    w = [s[:, m, g * P:(g + 1) * P] for s in (wqk_hi, wqk_lo)]
                    last = mm3(ps_q[:, m, :], w, xT_of(r))
                last.then_inc(q_psum, 1)

            def scores(b, r, k):
                wait_used(pe, square_done, b * PAIRS + k)
                for j in range(2):
                    h = 2 * k + j
                    pe.matmul(ps_s[:, j, 0:TB], k_stack[:, r, h, 0:P], q_stack[:, r, h, :], start=True, stop=True)
                    last = pe.matmul(ps_s[:, j, TB:SW], k_stack[:, r, h, P:TB], q_stack[:, r, h, P:TB],
                                     start=True, stop=True)
                last.then_inc(s_psum, 1)

            def prefix_v(b, r):
                wait_used(pe, yn_ready, b)
                for a in range(2):
                    va = [v_pad[:, r, t, 4 * a:4 * (a + 1), :].rearrange("p g c -> p (g c)") for t in range(NT)]
                    pe.matmul(ps_y[:, a, :], va[0], before[:, :], start=(a == 0), stop=False, skip_group_check=True)
                    pe.matmul(ps_y[:, a, P:TB], va[1], before[:, 0:P], start=False, stop=False, skip_group_check=True)

            def weigh_v(b, r, half):
                pe.wait_ge(mask_done, b * PAIRS + HALF * (half + 1))
                for j in range(2):
                    for t, cols in ((0, slice(0, TB)), (1, slice(TB, SW))):
                        for g in range(HALF):
                            k = HALF * half + g
                            if j == 0:
                                w = v_pad[:, r, t, k, 0:HD1]
                            else:
                                w = v_b[:, r, t, k, :]
                            dst = ps_y[VG * g:VG * g + HD1 * (j + 1), half, t * P:TB]
                            last = pe.matmul(dst, w, w_att[:, k, j, cols], start=False,
                                             stop=(half == 1 and j == 1 and t == 1), skip_group_check=True)
                last.then_inc(pv_done, 1)

            def hidden(b, r, e):
                wait_used(pe, silu_done, b * E + max(e - 1, 0))
                for c in range(NC):
                    w = [s[:, e, c * P:(c + 1) * P] for s in (ew1_hi, ew1_lo)]
                    last = mm3(ps_h[:, e % 2, c * TB:(c + 1) * TB], w, xT_of(r))
                last.then_inc(h_psum, 1)

            def expert_out(b, e):
                pe.wait_ge(h_lo_done, b * E + (e + 1))
                wait_used(pe, o_weighed, b * E + e)
                for c in range(NC):
                    w = [s[:, e * NC + c, :] for s in (ew2_hi, ew2_lo)]
                    last = mm3(ps_o[:, 0:TB], w, (h_hi[:, e % 2, c, :], h_lo[:, e % 2, c, :]),
                               start=(c == 0), stop=(c == NC - 1))
                last.then_inc(o_psum, 1)

            def num_T(b):
                pe.wait_ge(yn_ready, b + 1)
                pe.wait_ge(rest_done, b_groups(b))
                for t in range(NT):
                    for a in range(2):
                        last = pe.transpose(ps_q[:, t, a * P:(a + 1) * P], yn[:, a, t * P:(t + 1) * P], ident[:, :])
                last.then_inc(num_psum, 1)

            def b_groups(b):
                return min(NG * (b + 3), NG * B) if isinstance(b, int) else NG * (b + 3)

            def out_T(b, r, last_batch):
                pe.wait_ge(o_added, (b + 1) * (E - 1))
                if not last_batch:
                    pe.wait_ge(gateT_ready, b + 3)
                for t in range(NT):
                    last = pe.transpose(ps_t[:, t * P:(t + 1) * P], oT[:, r, t * P:(t + 1) * P], ident[:, :])
                last.then_inc(out_psum, 1)

            def y_T(b):
                pe.wait_ge(y_ready, b + 1)
                for t in range(NT):
                    last = pe.transpose(ps_q[:, 0, t * P:(t + 1) * P], y[:, t, :], ident[:, :])
                last.then_inc(yT_psum, 1)

            def attention_out(b):
                pe.wait_ge(yT_ready, b + 1)
                for t in range(NT):
                    last = pe.matmul(ps_q[:, 0, t * D:(t + 1) * D], yT[:, t * P:(t + 1) * P], wo_f[:, :],
                                     start=True, stop=True)
                last.then_inc(att_psum, 1)

            pe.wait_ge(const_step, 11)
            xT(0, 0)
            pe.wait_ge(w_split, 10)
            r1(0, 0)
            pe.wait_ge(small_in, 16 * SMALL_DMAS)
            logits(0, 0)
            for g in range(NG):
                qk(0, 0, g)
            v(0, 0)
            gate_T(0, 0)

            def batch(b, r, has_last, has_next):
                pe.wait_ge(stack_in, (b + 1) * (16 * STACK_DMAS))
                for k in range(PAIRS):
                    scores(b, r, k)
                    if k > 1:
                        if not has_last:
                            pe.wait_ge(ew2_lo_done, k - 1)
                        expert_out(b, k - 2)
                    elif has_last:
                        expert_out(b - 1, E - 2 + k)
                    if not has_last:
                        pe.wait_ge(ew1_lo_done, k + 1)
                    hidden(b, r, k)
                    if has_last:
                        if k == 1:
                            weigh_v(b - 1, 1 - r, 1)
                        if k == 3:
                            num_T(b - 1)
                        if k == 5:
                            y_T(b - 1)
                    if k == 3:
                        prefix_v(b, r)
                    if k == 4:
                        weigh_v(b, r, 0)
                    if has_next:
                        if k == 0:
                            xT(b + 1, 1 - r)
                        if k == 1:
                            r1(b + 1, 1 - r)
                        if k in (1, 2):
                            qk(b + 1, 1 - r, k - 1)
                        if k == 2:
                            logits(b + 1, 1 - r)
                        if k == 3:
                            v(b + 1, 1 - r)
                        if k == 5:
                            gate_T(b + 1, 1 - r)
                    if has_last and k == 6:
                        out_T(b - 1, 1 - r, not has_next)
                        attention_out(b - 1)

            for_batches(pe, batch)
            expert_out(B - 1, E - 2)
            weigh_v(B - 1, 1, 1)
            expert_out(B - 1, E - 1)
            num_T(B - 1)
            y_T(B - 1)
            out_T(B - 1, 1, True)
            attention_out(B - 1)


def kernel(**inputs):
    import numpy as np
    import concourse.bacc as bacc
    from concourse.bass_utils import run_bass_kernel_spmd

    g = {k: np.asarray(v) for k, v in inputs.items()}
    A, M = "L0_attn_", "L0_ffn_"
    E, _, HID = g[M + "ew1"].shape
    laid = {
        "x": g[A + "hidden_states"],
        "wqT": g[A + "Wq"].T, "wkT": g[A + "Wk"].T, "wvT": g[A + "Wv"].T, "woT": g[A + "Wo"].T,
        "rw1": g[M + "rw1"], "rb1": g[M + "rb1"].reshape(-1, 1),
        "rw2": g[M + "rw2"], "rb2": g[M + "rb2"].reshape(1, -1),
        "ew1": g[M + "ew1"],
        "eb1": g[M + "eb1"].reshape(E * (HID // P), P).T,
        "ew2": g[M + "ew2"], "eb2": g[M + "eb2"].T,
    }
    nc = bacc.Bacc("TRN2", target_bir_lowering=False, num_devices=1)
    arrays, args = {}, []
    for name, a in laid.items():
        arrays[name] = np.ascontiguousarray(a)
        args.append(nc.dram_tensor(name, a.shape, mybir.dt.from_np(a.dtype), kind="ExternalInput").ap())
    args.append(nc.dram_tensor("out", laid["x"].shape, F32, kind="ExternalOutput").ap())
    fused_layer(nc, *args)
    r = run_bass_kernel_spmd(nc, [arrays], core_ids=[0])
    return r.results[0]["out"]
```

```python
import itertools
from contextlib import ExitStack

import concourse.bass as bass
from concourse import mybir

F32 = mybir.dt.float32
F32R = mybir.dt.float32r
BF16 = mybir.dt.bfloat16
I32 = mybir.dt.int32
U32 = mybir.dt.uint32
ALU = mybir.AluOpType
ACT = mybir.ActivationFunctionType

P = 128
RD = 4.0
EPS_LN = 1e-5
EPS_DEN = 1e-12


def fused_layer(nc, x, wqT, wkT, wvT, woT, rw1, rb1, rw2, rb2, ew1, eb1, ew2, eb2, out):
    B, TB, D = x.shape
    NT = TB // P
    TILES = B * NT
    FD = 16
    H = wqT.shape[1] // FD
    HD = D // H
    HD1 = HD + 1
    E, _, HID = ew1.shape
    NC = HID // P
    PAIRS = H // 2
    NG = H * FD // P
    Q_RUNS = ((0, 1, 2), (0, 1), (0,))
    K_RUNS = ((0,), (0,), (0, 1), (1, 2))
    KS = FD * 6
    STACK_DMAS = len(Q_RUNS) + len(K_RUNS)
    SW = TB + P
    VG = 32
    VROWS = NT * 4
    assert D == P and NT == 2 and PAIRS == E and NC == 2 and NG == 2

    x_v = x.rearrange("b (t p) d -> p (b t) d", p=P)
    out_v = out.rearrange("b (t p) d -> p (b t) d", p=P)
    parts_d = nc.dram_tensor("parts_scratch", (2, NG, 2, 3, P, TB), BF16, kind="Internal").ap()
    gate_d = nc.dram_tensor("gate_scratch", (2, E, TB), F32, kind="Internal").ap()

    with ExitStack() as ctx:
        def sb(name, shape, dt=F32):
            return ctx.enter_context(nc.sbuf_tensor(name, shape, dt))

        def bank(name, shape):
            return ctx.enter_context(nc.psum_tensor(name, shape, F32))

        def sem(name):
            return ctx.enter_context(nc.semaphore(name))

        ident = sb("ident", [P, P])
        silu_out = sb("silu_out", [P, 1])
        before = sb("before", [P, TB])
        before_r = sb("before_r", [P, TB], F32R)
        iota8 = sb("iota8", [P, E])
        den_row = sb("den_row", [P, 8, VG])
        wq_f = sb("wq_f", [P, H * FD])
        wk_f = sb("wk_f", [P, H * FD])
        wv_f = sb("wv_f", [P, D])
        wo_f = sb("wo_f", [P, D])
        rw1_f = sb("rw1_f", [P, D])
        rw2_f = sb("rw2_f", [P, E])
        rb1_c = sb("rb1_c", [P, 1])
        rb2_b = sb("rb2_b", [P, E])
        eb1_c = sb("eb1_c", [P, E * NC])
        eb2_c = sb("eb2_c", [P, E])
        ew1_f = sb("ew1_f", [P, E, HID])
        ew2_f = sb("ew2_f", [P, E * NC, D])
        wqk_hi = sb("wqk_hi", [P, 2, H * FD], F32R)
        wqk_lo = sb("wqk_lo", [P, 2, H * FD], F32R)
        wv_hi = sb("wv_hi", [P, 8, VG], F32R)
        wv_lo = sb("wv_lo", [P, 8, VG], F32R)
        rw1_hi = sb("rw1_hi", [P, D], F32R)
        rw1_lo = sb("rw1_lo", [P, D], F32R)
        ew1_hi = sb("ew1_hi", [P, E, HID], F32R)
        ew1_lo = sb("ew1_lo", [P, E, HID], F32R)
        ew2_hi = sb("ew2_hi", [P, E * NC, D], F32R)
        ew2_lo = sb("ew2_lo", [P, E * NC, D], F32R)

        x_all = sb("x_all", [P, TILES, D])
        stats = sb("stats", [P, TILES, 6])
        mv = sb("mv", [P, TILES, 2])
        var_eps = sb("var_eps", [P, TILES])
        rstd0 = sb("rstd0", [P, TILES])
        minus_half = sb("minus_half", [P, TILES])
        newton = sb("newton", [P, TILES])
        rstd = sb("rstd", [P, TILES])
        xn = sb("xn", [P, 2, NT, D])
        xT_hi = sb("xT_hi", [P, 2, TB], F32R)
        xT_lo = sb("xT_lo", [P, 2, TB], F32R)
        q_stack = sb("q_stack", [KS, 2, H, TB], BF16)
        k_stack = sb("k_stack", [KS, 2, H, TB], BF16)
        v_pad = sb("v_pad", [P, 2, NT, 8, VG])
        v_b = sb("v_b", [P, 2, NT, 8, 2 * HD1])
        v0_hi = sb("v0_hi", [P, 8 * VG], F32R)
        v0_lo = sb("v0_lo", [P, 8 * VG], F32R)
        r1T = sb("r1T", [P, 2, TB])
        gate = sb("gate", [P, 2, NT, E])
        oT = sb("oT", [P, 2, TB])
        gate_b = sb("gate_b", [P, 2, E, TB])
        parts = sb("parts", [P, NG, 2, 3, TB], BF16)
        rest = sb("rest", [P, NG, 2, TB])
        gateT = sb("gateT", [E, TB])
        w_att = sb("w_att", [P, PAIRS, 2, SW])
        yn = sb("yn", [P, 2, TB])
        y = sb("y", [P, NT, D])
        yT = sb("yT", [P, TB])
        h_f = sb("h_f", [P, 2, NC, TB])
        weighed = sb("weighed", [P, 2, TB])
        h_hi = sb("h_hi", [P, 2, NC, TB], F32R)
        h_lo = sb("h_lo", [P, 2, NC, TB], F32R)
        lg = sb("lg", [P, NT, E])
        top = sb("top", [P, NT, 8])
        topi = sb("topi", [P, NT, 8], U32)
        topf = sb("topf", [P, NT, 2])
        gap = sb("gap", [P, NT])
        th = sb("th", [P, NT])
        w12 = sb("w12", [P, NT, 2])
        hot = sb("hot", [P, NT, 2, E])
        hotw = sb("hotw", [P, NT, 2, E])
        den = sb("den", [P, VROWS * 2, 2])
        rden = sb("rden", [P, VROWS * 2, 2])

        ps_s = bank("ps_s", [P, 2, 512])
        ps_h = bank("ps_h", [P, 2, 512])
        ps_o = bank("ps_o", [P, 512])
        ps_y = bank("ps_y", [P, 2, TB])
        ps_t = bank("ps_t", [P, 512])
        ps_q = bank("ps_q", [P, 2, TB])

        first_x_in = sem("first_x_in")
        other_x_in = sem("other_x_in")
        proj_in = [sem(f"proj_in{n}") for n in range(4)]
        small_in = sem("small_in")
        late_in = sem("late_in")
        ew1_in = sem("ew1_in")
        ew2_in = [sem(f"ew2_in{half}") for half in range(2)]
        const_step = sem("const_step")
        w_hi_done = sem("w_hi_done")
        w_lo_done = sem("w_lo_done")
        ew1_hi_done = sem("ew1_hi_done")
        ew1_lo_done = sem("ew1_lo_done")
        ew2_hi_done = sem("ew2_hi_done")
        ew2_lo_done = sem("ew2_lo_done")
        ln_step = sem("ln_step")
        var_done = sem("var_done")
        pow_done = sem("pow_done")
        xn_ready = sem("xn_ready")
        residual_ready = sem("residual_ready")
        xT_psum = sem("xT_psum")
        xT_hi_done = sem("xT_hi_done")
        xT_lo_done = sem("xT_lo_done")
        r1_psum = sem("r1_psum")
        r1_ready = sem("r1_ready")
        lg_psum = sem("lg_psum")
        lg_read = sem("lg_read")
        route_step = sem("route_step")
        tanh_done = sem("tanh_done")
        gate_ready = sem("gate_ready")
        gateT_psum = sem("gateT_psum")
        gateT_ready = sem("gateT_ready")
        gate_stored = sem("gate_stored")
        gate_in = sem("gate_in")
        v_psum = sem("v_psum")
        v_ready = sem("v_ready")
        q_psum = sem("q_psum")
        part_h_done = sem("part_h_done")
        rest_done = sem("rest_done")
        part_m_done = sem("part_m_done")
        parts_ready = sem("parts_ready")
        parts_stored = [sem(f"parts_stored{g}") for g in range(NG)]
        stack_in = [sem(f"stack_in{g}") for g in range(NG)]
        s_psum = sem("s_psum")
        square_done = sem("square_done")
        mask_done = sem("mask_done")
        v0_hi_done = sem("v0_hi_done")
        v0_lo_done = sem("v0_lo_done")
        prefix_done = sem("prefix_done")
        pv_done = sem("pv_done")
        h_psum = sem("h_psum")
        silu_done = sem("silu_done")
        h_hi_done = sem("h_hi_done")
        act_h_hi_done = sem("act_h_hi_done")
        h_lo_done = sem("h_lo_done")
        o_psum = sem("o_psum")
        o_weighed = sem("o_weighed")
        o_added = sem("o_added")
        yn_ready = sem("yn_ready")
        num_psum = sem("num_psum")
        den_step = sem("den_step")
        y_ready = sem("y_ready")
        out_psum = sem("out_psum")
        sum_added = sem("sum_added")
        yT_psum = sem("yT_psum")
        yT_ready = sem("yT_ready")
        out_stored = sem("out_stored")

        ROUTE_STEPS = 9
        ACT_SPLITS = (3, 4, 7)
        HALF = PAIRS // 2
        STATISTICS = (0, 1, 3, 4)
        POWERS = (2, 5)
        LATER = [2 * NT + n * (TILES - 2 * NT) // 4 for n in range(5)]
        SMALL_DMAS = 3
        proj = [(wqk_hi[:, 0, :], wqk_lo[:, 0, :], wq_f[:, :]), (wqk_hi[:, 1, :], wqk_lo[:, 1, :], wk_f[:, :]),
                (rw1_hi[:, :], rw1_lo[:, :], rw1_f[:, :])]
        wv_pairs = wv_f[:, :].rearrange("p (g i d) -> p g i d", i=2, d=HD)
        proj += [(wv_hi[:, :, i * HD1:i * HD1 + HD], wv_lo[:, :, i * HD1:i * HD1 + HD], wv_pairs[:, :, i, :])
                 for i in range(2)]

        def for_batches(eng, batch):
            batch(0, 0, False, True)
            with eng.Fori(0, B // 2 - 1) as i:
                batch(i * 2 + 1, 1, True, True)
                batch(i * 2 + 2, 0, True, True)
            batch(B - 1, 1, True, False)

        def wait_used(eng, what, n):
            if not isinstance(n, int) or n > 0:
                eng.wait_ge(what, n)

        def qk_psum(b, g):
            return ps_y[:, :, :] if isinstance(b, int) and b == 0 and g == 1 else ps_q[:, :, :]

        block = ctx.enter_context(nc.Block())

        @block.sync
        def _(sp):
            sp.dma_start(x_all[:, 0:NT, :], x_v[:, 0:NT, :]).then_inc(first_x_in, 16)
            for n, (dst, src) in enumerate(((wq_f, wqT), (wk_f, wkT), (rw1_f, rw1), (wv_f, wvT))):
                sp.dma_start(dst[:, :], src).then_inc(proj_in[n], 16)
            for dst, src in ((rb1_c, rb1), (rw2_f, rw2), (rb2_b, rb2.to_broadcast([P, E]))):
                sp.dma_start(dst[:, :], src).then_inc(small_in, 16)
            sp.dma_start(x_all[:, NT:TILES, :], x_v[:, NT:TILES, :]).then_inc(other_x_in, 16)
            sp.dma_start(ew1_f[:, :, :], ew1.rearrange("e d h -> d e h")).then_inc(ew1_in, 16)

            for dst, src in ((eb1_c, eb1), (eb2_c, eb2), (wo_f, woT)):
                sp.dma_start(dst[:, :], src).then_inc(late_in, 16)

            def load_ew2(half):
                experts = slice(half * E // 2, (half + 1) * E // 2)
                sp.dma_start(ew2_f[:, NC * experts.start:NC * experts.stop, :],
                             ew2[experts, :, :].rearrange("e (c p) d -> p (e c) d", p=P)).then_inc(ew2_in[half], 16)

            def store_parts(b, r):
                for g in range(NG):
                    wait_used(sp, stack_in[g], b * (16 * STACK_DMAS))
                    sp.nop(nofuse=True)
                    sp.wait_ge(parts_ready, b * NG + (g + 1))
                    sp.nop(nofuse=True)
                    sp.dma_start(parts_d[r, g, :, :, :, :].rearrange("m s p t -> p (m s) t"),
                                 parts[:, g, :, :, :].rearrange("p m s t -> p (m s) t")).then_inc(parts_stored[g], 16)

            def load_stack(b, r, g, used):
                sp.wait_ge(parts_stored[g], (b + 1) * 16)
                sp.nop(nofuse=True)
                if g == 0:
                    wait_used(sp, s_psum, used)
                    sp.nop(nofuse=True)
                for stack, m, runs in ((q_stack, 0, Q_RUNS), (k_stack, 1, K_RUNS)):
                    row = 0
                    for run in runs:
                        rows = FD * len(run)
                        sp.dma_start(stack[row:row + rows, r, g * 8:(g + 1) * 8, :].rearrange("p h t -> p (h t)"),
                                     parts_d[r, g, m, run[0]:run[-1] + 1, :, :].rearrange(
                                         "s (f h) t -> (s f) (h t)", f=FD)).then_inc(stack_in[g], 16)
                        row += rows

            def spread_gate(b, r, used):
                sp.wait_ge(gateT_ready, b + 1)
                sp.nop(nofuse=True)
                wait_used(sp, gate_in, b * 16)
                sp.nop(nofuse=True)
                sp.dma_start(gate_d[r, :, :], gateT[:, :]).then_inc(gate_stored, 16)
                sp.wait_ge(gate_stored, (b + 1) * 16)
                sp.nop(nofuse=True)
                wait_used(sp, o_weighed, used)
                sp.nop(nofuse=True)
                sp.dma_start(gate_b[:, r, :, :].rearrange("p e t -> p (e t)"),
                             gate_d[r:r + 1, :, :].rearrange("o e t -> o (e t)").to_broadcast([P, E * TB])
                             ).then_inc(gate_in, 16)

            def store(b):
                sp.wait_ge(sum_added, b + 2)
                sp.nop(nofuse=True)
                sp.dma_start(out_v[:, bass.ds(b * NT, NT), :], x_all[:, bass.ds(b * NT, NT), :]).then_inc(out_stored, 16)

            store_parts(0, 0)
            load_ew2(0)
            load_stack(0, 0, 0, 0)
            spread_gate(0, 0, 0)
            load_stack(0, 0, 1, 0)
            load_ew2(1)

            def batch(b, r, has_last, has_next):
                if has_next:
                    store_parts(b + 1, 1 - r)
                    for g in range(NG):
                        load_stack(b + 1, 1 - r, g, b * PAIRS)
                    spread_gate(b + 1, 1 - r, b * E)
                if has_last:
                    store(b - 1)

            for_batches(sp, batch)
            store(B - 1)
            sp.wait_ge(out_stored, 16 * B)

        @block.gpsimd
        def _(pool):
            pool.memset(minus_half[:, :], -0.5).then_inc(const_step, 1)
            pool.memset(ident[:, :], 0.0).then_inc(const_step, 1)
            pool.memset(before[:, :], 1.0).then_inc(const_step, 1)
            pool.memset(den_row[:, :, :], 0.0).then_inc(const_step, 1)
            pool.wait_ge(const_step, 4)
            pool.affine_select(out=ident[:, :], in_=ident[:, :], compare_op=ALU.not_equal, fill=1.0,
                               base=0, pattern=[[-1, P]], channel_multiplier=1).then_inc(const_step, 1)
            pool.affine_select(out=before[:, 0:P], in_=before[:, 0:P], compare_op=ALU.is_ge, fill=0.0,
                               base=0, pattern=[[1, P]], channel_multiplier=-1).then_inc(const_step, 1)
            pool.memset(den_row[:, :, HD:2 * HD1:HD1], 1.0).then_inc(const_step, 1)
            for w in (wv_hi, wv_lo):
                pool.memset(w[:, :, :].bitcast(F32), 0.0).then_inc(const_step, 1)
            pool.memset(v_b[:, :, :, :, :], 0.0).then_inc(const_step, 1)
            pool.iota(iota8[:, :], pattern=[[1, E]], base=0, channel_multiplier=0,
                      allow_small_or_imprecise_dtypes=True).then_inc(const_step, 1)
            pool.wait_ge(const_step, 6)
            pool.tensor_copy(before_r[:, :], before[:, :]).then_inc(const_step, 1)

            def residual(b, r):
                pool.wait_ge(xn_ready, NT * (b + 1))
                pool.nop(nofuse=True)
                pool.tensor_tensor(x_all[:, bass.ds(b * NT, NT), :], x_all[:, bass.ds(b * NT, NT), :],
                                   xn[:, r, :, :], ALU.add).then_inc(residual_ready, 1)

            def part_l(b, g):
                pool.wait_ge(part_m_done, b * NG + (g + 1))
                pool.tensor_tensor(parts[:, g, :, 2, :], rest[:, g, :, :], parts[:, g, :, 1, :],
                                   ALU.subtract).then_inc(parts_ready, 1)

            def power(t0, t1, n):
                pool.wait_ge(var_done, n)
                pool.tensor_tensor(rstd0[:, t0:t1], var_eps[:, t0:t1], minus_half[:, t0:t1],
                                   ALU.pow).then_inc(pow_done, 1)

            def low_weights(e):
                pool.wait_ge(ew2_hi_done, e + 1)
                pool.tensor_tensor(ew2_lo[:, NC * e:NC * (e + 1), :], ew2_f[:, NC * e:NC * (e + 1), :],
                                   ew2_hi[:, NC * e:NC * (e + 1), :].bitcast(F32),
                                   ALU.subtract).then_inc(ew2_lo_done, 1)

            def mask(b, k):
                pool.wait_ge(square_done, b * PAIRS + (k + 1))
                pool.nop(nofuse=True)
                for j in range(2):
                    diag = w_att[:, k, j, :].rearrange("p (n q) -> p n q", q=P)[:, 0:3:2, :]
                    last = pool.affine_select(out=diag, in_=diag, compare_op=ALU.is_ge, fill=0.0, base=0,
                                              pattern=[[0, 2], [1, P]], channel_multiplier=-1)
                last.then_inc(mask_done, 1)

            def add_expert(b, r, e):
                pool.wait_ge(o_weighed, b * E + (e + 1))
                if e > 1:
                    pool.wait_ge(o_added, b * (E - 1) + (e - 1))
                pool.tensor_tensor(oT[:, r, :], oT[:, r, :], weighed[:, e % 2, :], ALU.add).then_inc(o_added, 1)

            power(0, NT, 1)
            for n, (hi, lo, w) in enumerate(proj):
                pool.wait_ge(w_hi_done, n + 1)
                pool.tensor_tensor(lo, w, hi.bitcast(F32), ALU.subtract).then_inc(w_lo_done, 1)
            power(NT, 2 * NT, 2)
            for e in range(E // 2):
                low_weights(e)

            def batch(b, r, has_last, has_next):
                for k in range(PAIRS):
                    if has_next and k == 3:
                        part_l(b + 1, 1)
                    if not has_last and k in POWERS:
                        n = POWERS.index(k)
                        power(LATER[2 * n], LATER[2 * n + 2], 4 + 2 * n)
                    if not has_last and 3 <= k < 3 + E // 2:
                        low_weights(E // 2 + k - 3)
                    mask(b, k)
                    if k >= 3:
                        add_expert(b, r, k - 2)
                    elif has_last and k < 2:
                        add_expert(b - 1, 1 - r, E - 2 + k)
                    if has_next and k == 2:
                        part_l(b + 1, 0)
                    if k == 1:
                        residual(b, r)

            for_batches(pool, batch)
            add_expert(B - 1, 1, E - 2)
            add_expert(B - 1, 1, E - 1)

        @block.scalar
        def _(act):
            def split_proj(n):
                if n < len(proj_in):
                    act.wait_ge(proj_in[n], 16)
                if n == 3:
                    act.wait_ge(const_step, 9)
                act.activation(proj[n][0], proj[n][2], ACT.Copy).then_inc(w_hi_done, 1)

            def split_ew1(e):
                act.activation(ew1_hi[:, e, :], ew1_f[:, e, :], ACT.Copy).then_inc(ew1_hi_done, 1)

            def split_ew2(e):
                act.activation(ew2_hi[:, NC * e:NC * (e + 1), :], ew2_f[:, NC * e:NC * (e + 1), :],
                               ACT.Copy).then_inc(ew2_hi_done, 1)

            def xT(b, r):
                act.wait_ge(xT_psum, b + 1)
                act.activation(xT_hi[:, r, :], ps_t[:, 0:TB], ACT.Copy).then_inc(xT_hi_done, 1)

            def part_h(b, g):
                act.wait_ge(q_psum, b * NG + (g + 1))
                wait_used(act, parts_stored[g], b * 16)
                act.activation(parts[:, g, :, 0, :], qk_psum(b, g), ACT.Copy).then_inc(part_h_done, 1)

            def part_m(b, g):
                act.wait_ge(rest_done, b * NG + (g + 1))
                act.activation(parts[:, g, :, 1, :], rest[:, g, :, :], ACT.Copy).then_inc(part_m_done, 1)

            def r1(b, r):
                act.wait_ge(r1_psum, b + 1)
                act.activation(r1T[:, r, :], ps_t[:, 0:TB], ACT.Silu, bias=rb1_c[:, 0:1]).then_inc(r1_ready, 1)

            def tanh(b):
                act.wait_ge(route_step, b * ROUTE_STEPS + 7)
                act.activation(th[:, :], gap[:, :], ACT.Tanh, scale=0.5).then_inc(tanh_done, 1)

            def gate_T(b):
                act.wait_ge(gateT_psum, b + 1)
                wait_used(act, gate_stored, b * 16)
                act.activation(gateT[:, :], ps_t[0:E, 0:TB], ACT.Copy).then_inc(gateT_ready, 1)

            act.wait_ge(const_step, 1)
            act.activation(silu_out[:, :], minus_half[:, 0:1], ACT.Silu)
            split_proj(0)
            split_proj(1)
            xT(0, 0)
            split_proj(2)
            split_proj(3)
            split_proj(4)
            part_h(0, 0)
            part_m(0, 0)
            part_h(0, 1)
            part_m(0, 1)
            act.wait_ge(small_in, 16 * SMALL_DMAS)
            r1(0, 0)
            act.wait_ge(ew1_in, 16)
            split_ew1(0)
            split_ew1(1)
            tanh(0)
            for e in range(2, E):
                split_ew1(e)
            act.wait_ge(ew2_in[0], 16)
            for e in range(E // 2):
                split_ew2(e)
            gate_T(0)
            xT(1, 1)
            act.wait_ge(late_in, 16 * 3)

            def v0_high(b, r):
                act.wait_ge(v_ready, b + 1)
                wait_used(act, prefix_done, b)
                act.activation(v0_hi[:, :], v_pad[:, r, 0, :, :].rearrange("p g c -> p (g c)"),
                               ACT.Copy).then_inc(v0_hi_done, 1)

            def square(b, k):
                act.wait_ge(s_psum, b * PAIRS + (k + 1))
                if k % HALF == 0:
                    wait_used(act, pv_done, b * 2 - 1 + k // HALF)
                act.activation(w_att[:, k, :, :], ps_s[:, :, 0:SW], ACT.Square, bias=1.0,
                               scale=1.0 / RD).then_inc(square_done, 1)

            def silu(b, e):
                act.wait_ge(h_psum, b * E + (e + 1))
                wait_used(act, h_lo_done, b * E + max(e - 1, 0))
                for c in range(NC):
                    last = act.activation(h_f[:, e % 2, c, :], ps_h[:, e % 2, c * TB:(c + 1) * TB], ACT.Silu,
                                          bias=eb1_c[:, e * NC + c:e * NC + c + 1])
                last.then_inc(silu_done, 1)
                if e in ACT_SPLITS:
                    act.wait_ge(silu_done, b * E + (e + 1))
                    wait_used(act, o_psum, b * E + max(e - 1, 0))
                    act.activation(h_hi[:, e % 2, :, :], h_f[:, e % 2, :, :], ACT.Copy).then_inc(act_h_hi_done, 1)

            def leave(b):
                act.wait_ge(pv_done, b * 2 + 2)
                wait_used(act, num_psum, b)
                act.activation(yn[:, :, :], ps_y[:, :, :], ACT.Copy).then_inc(yn_ready, 1)

            def y_T(b):
                act.wait_ge(yT_psum, b + 1)
                wait_used(act, out_psum, b)
                act.activation(yT[:, :], ps_q[:, 0, :], ACT.Copy).then_inc(yT_ready, 1)

            def batch(b, r, has_last, has_next):
                for k in range(PAIRS):
                    if has_next and k in (2, 3):
                        part_m(b + 1, k - 2)
                    square(b, k)
                    if has_next and k == 2:
                        part_h(b + 1, 1)
                    silu(b, k)
                    if not has_last and 3 <= k < 3 + E // 2:
                        if k == 3:
                            act.wait_ge(ew2_in[1], 16)
                        split_ew2(E // 2 + k - 3)
                    if has_next:
                        if has_last and k == 0:
                            xT(b + 1, 1 - r)
                        if k == 1:
                            part_h(b + 1, 0)
                            r1(b + 1, 1 - r)
                        if k == 3:
                            tanh(b + 1)
                        if k == 5:
                            gate_T(b + 1)
                        if k == 6:
                            v0_high(b + 1, 1 - r)
                    if not has_last and k == 0:
                        v0_high(b, r)
                    if has_last:
                        if k == 1:
                            leave(b - 1)
                        if k == 5:
                            y_T(b - 1)

            for_batches(act, batch)
            leave(B - 1)
            y_T(B - 1)

        @block.vector
        def _(dve):
            ln_steps = itertools.count(1)

            def ordered(instruction):
                instruction.then_inc(ln_step, 1)
                dve.wait_ge(ln_step, next(ln_steps))

            def variance(t0, t1):
                for t in range(t0, t1):
                    last = dve.bn_stats(stats[:, t, :], x_all[:, t, :])
                ordered(last)
                for t in range(t0, t1):
                    last = dve.bn_aggr(mv[:, t, :], stats[:, t, :])
                ordered(last)
                dve.tensor_scalar(var_eps[:, t0:t1], mv[:, t0:t1, 1], EPS_LN, None, ALU.add).then_inc(var_done, 1)

            def deviation(t0, t1, n):
                dve.wait_ge(pow_done, n)
                s, v, c = rstd0[:, t0:t1], var_eps[:, t0:t1], newton[:, t0:t1]
                ordered(dve.tensor_tensor(c, s, s, ALU.mult))
                ordered(dve.tensor_tensor(c, c, v, ALU.mult))
                ordered(dve.tensor_scalar(c, c, -0.5, 1.5, ALU.mult, ALU.add))
                ordered(dve.tensor_tensor(rstd[:, t0:t1], s, c, ALU.mult))

            def normalise(b, r):
                for t in range(NT):
                    dve.tensor_scalar(xn[:, r, t, :], x_all[:, bass.ds(b * NT + t, 1), :].squeeze(1),
                                      mv[:, bass.ds(b * NT + t, 1), 0:1].squeeze(1),
                                      rstd[:, bass.ds(b * NT + t, 1)],
                                      ALU.subtract, ALU.mult).then_inc(xn_ready, 1)

            dve.wait_ge(first_x_in, 16)
            variance(0, NT)
            deviation(0, NT, 1)
            normalise(0, 0)

            def split_ew1(e):
                dve.wait_ge(ew1_hi_done, e + 1)
                dve.tensor_tensor(ew1_lo[:, e, :], ew1_f[:, e, :], ew1_hi[:, e, :].bitcast(F32),
                                  ALU.subtract).then_inc(ew1_lo_done, 1)

            def xT(b, r):
                dve.wait_ge(xT_hi_done, b + 1)
                dve.tensor_tensor(xT_lo[:, r, :], ps_t[:, 0:TB], xT_hi[:, r, :].bitcast(F32),
                                  ALU.subtract).then_inc(xT_lo_done, 1)

            def qk_rest(b, g):
                dve.wait_ge(part_h_done, b * NG + (g + 1))
                wait_used(dve, parts_ready, (b - 1) * NG + (g + 1))
                dve.tensor_tensor(rest[:, g, :, :], qk_psum(b, g), parts[:, g, :, 0, :],
                                  ALU.subtract).then_inc(rest_done, 1)

            def v0_low(b, r):
                dve.wait_ge(v0_hi_done, b + 1)
                dve.tensor_tensor(v0_lo[:, :], v_pad[:, r, 0, :, :].rearrange("p g c -> p (g c)"),
                                  v0_hi[:, :].bitcast(F32), ALU.subtract).then_inc(v0_lo_done, 1)

            def route_choose(b):
                def step(n):
                    dve.wait_ge(route_step, b * ROUTE_STEPS + n)

                dve.wait_ge(lg_psum, b + 1)
                dve.tensor_tensor(lg[:, :, :], ps_t[:, 0:NT * E].rearrange("p (t e) -> p t e", e=E),
                                  rb2_b[:, :].unsqueeze(1).to_broadcast([P, NT, E]), ALU.add).then_inc(lg_read, 1)
                dve.wait_ge(lg_read, b + 1)
                dve.nop(nofuse=True)
                for t in range(NT):
                    dve.max(top[:, t, :], lg[:, t, :]).then_inc(route_step, 1)
                step(2)
                dve.tensor_tensor(gap[:, :], top[:, :, 0], top[:, :, 1], ALU.subtract)
                for t in range(NT):
                    dve.max_index(topi[:, t, :], top[:, t, :], lg[:, t, :]).then_inc(route_step, 1)
                step(4)
                dve.tensor_copy(topf[:, :, :], topi[:, :, 0:2]).then_inc(route_step, 1)
                step(5)
                dve.tensor_tensor(hot[:, :, :, :].rearrange("p t j e -> p (t j) e"),
                                  iota8[:, :].unsqueeze(1).to_broadcast([P, NT * 2, E]),
                                  topf[:, :, :].rearrange("p t j -> p (t j)").unsqueeze(2).to_broadcast([P, NT * 2, E]),
                                  ALU.is_equal).then_inc(route_step, 2)

            def route_weigh(b, r):
                dve.wait_ge(tanh_done, b + 1)
                dve.tensor_scalar(w12[:, :, 0], th[:, :], 0.5, 0.5, ALU.mult, ALU.add)
                dve.tensor_scalar(w12[:, :, 1], th[:, :], -0.5, 0.5, ALU.mult, ALU.add).then_inc(route_step, 1)
                dve.wait_ge(route_step, b * ROUTE_STEPS + 8)
                dve.tensor_tensor(hotw[:, :, :, :].rearrange("p t j e -> p (t j) e"),
                                  hot[:, :, :, :].rearrange("p t j e -> p (t j) e"),
                                  w12[:, :, :].rearrange("p t j -> p (t j)").unsqueeze(2).to_broadcast([P, NT * 2, E]),
                                  ALU.mult).then_inc(route_step, 1)
                dve.wait_ge(route_step, b * ROUTE_STEPS + 9)
                dve.tensor_tensor(gate[:, r, :, :], hotw[:, :, 0, :], hotw[:, :, 1, :],
                                  ALU.add).then_inc(gate_ready, 1)

            def v(b, r):
                dve.wait_ge(v_psum, b + 1)
                dve.tensor_tensor(v_b[:, r, :, :, HD1:2 * HD1].rearrange("p t g d -> p (t g) d"),
                                  ps_t[:, :].rearrange("p (n c) -> p n c", c=VG)[:, :, HD1:2 * HD1],
                                  den_row[:, 0:1, HD1:2 * HD1].to_broadcast([P, NT * 8, HD1]), ALU.add)
                dve.tensor_tensor(v_pad[:, r, :, :, :].rearrange("p t g c -> p t (g c)"),
                                  ps_t[:, :].rearrange("p (t c) -> p t c", t=NT),
                                  den_row[:, :, :].rearrange("p g c -> p (g c)").unsqueeze(1).to_broadcast([P, NT, 8 * VG]),
                                  ALU.add).then_inc(v_ready, 1)

            xT(0, 0)
            dve.wait_ge(const_step, 12)
            for g in range(NG):
                qk_rest(0, g)
                dve.wait_ge(part_m_done, g + 1)
                dve.tensor_tensor(parts[:, g, :, 2, :], rest[:, g, :, :], parts[:, g, :, 1, :],
                                  ALU.subtract).then_inc(parts_ready, 1)
            dve.wait_ge(small_in, 16 * SMALL_DMAS)
            dve.wait_ge(other_x_in, 16)
            route_choose(0)
            split_ew1(0)
            variance(NT, 2 * NT)
            route_weigh(0, 0)
            v(0, 0)
            split_ew1(1)
            deviation(NT, 2 * NT, 2)
            normalise(1, 1)
            for e in range(2, E):
                split_ew1(e)
            xT(1, 1)
            dve.wait_ge(late_in, 16 * 3)
            dve.nop(nofuse=True).then_inc(sum_added, 1)

            def split_h(b, e):
                dve.wait_ge(silu_done, b * E + (e + 1))
                wait_used(dve, o_psum, b * E + max(e - 1, 0))
                by_act = sum(n < e for n in ACT_SPLITS)
                if e in ACT_SPLITS:
                    dve.wait_ge(act_h_hi_done, b * len(ACT_SPLITS) + (by_act + 1))
                else:
                    dve.tensor_copy(h_hi[:, e % 2, :, :], h_f[:, e % 2, :, :]).then_inc(h_hi_done, 1)
                    dve.wait_ge(h_hi_done, b * (E - len(ACT_SPLITS)) + (e - by_act + 1))
                dve.tensor_tensor(h_lo[:, e % 2, :, :], h_f[:, e % 2, :, :], h_hi[:, e % 2, :, :].bitcast(F32),
                                  ALU.subtract).then_inc(h_lo_done, 1)

            def weigh(b, r, e):
                if e == 0:
                    dve.wait_ge(gate_in, (b + 1) * 16)
                    dst = oT[:, r, :]
                else:
                    dst = weighed[:, e % 2, :]
                    if e > 2:
                        dve.wait_ge(o_added, b * (E - 1) + (e - 2))
                    else:
                        wait_used(dve, o_added, b * (E - 1))
                dve.wait_ge(o_psum, b * E + (e + 1))
                dve.scalar_tensor_tensor(out=dst, in0=ps_o[:, 0:TB], scalar=eb2_c[:, e:e + 1],
                                         in1=gate_b[:, r, e, :], op0=ALU.add, op1=ALU.mult).then_inc(o_weighed, 1)

            def divide(b):
                dve.wait_ge(num_psum, b + 1)
                num = ps_q[:, :, :].rearrange("p t (g c) -> p (t g) c", c=VG)[:, :, 0:2 * HD1].rearrange(
                    "p g (i d) -> p g i d", d=HD1)
                dve.tensor_scalar(den[:, :, :], num[:, :, :, HD], 2 * EPS_DEN, None, ALU.add).then_inc(den_step, 1)
                dve.wait_ge(den_step, b * 2 + 1)
                dve.reciprocal(rden[:, :, :], den[:, :, :]).then_inc(den_step, 1)
                dve.wait_ge(den_step, b * 2 + 2)
                dve.tensor_tensor(y[:, :, :].rearrange("p t (g i d) -> p (t g) i d", i=2, d=HD), num[:, :, :, 0:HD],
                                  rden[:, :, :].unsqueeze(3).to_broadcast([P, VROWS * 2, 2, HD]),
                                  ALU.mult).then_inc(y_ready, 1)

            def add_out(b):
                dve.wait_ge(out_psum, b + 1)
                dve.wait_ge(residual_ready, b + 1)
                dve.nop(nofuse=True)
                res = x_all[:, bass.ds(b * NT, NT), :]
                dve.tensor_tensor(res, ps_t[:, 0:TB].rearrange("p (t d) -> p t d", d=D), res,
                                  ALU.add).then_inc(sum_added, 1)

            def batch(b, r, has_last, has_next):
                for k in range(PAIRS):
                    if has_last and has_next and k == 0:
                        dve.wait_ge(residual_ready, b)
                        dve.wait_ge(xT_psum, b)
                        normalise(b + 1, 1 - r)
                    if k > 0:
                        split_h(b, k - 1)
                    elif has_last:
                        split_h(b - 1, E - 1)
                    if k > 1:
                        weigh(b, r, k - 2)
                    elif has_last:
                        weigh(b - 1, 1 - r, E - 2 + k)
                    if has_next:
                        if has_last and k == 0:
                            xT(b + 1, 1 - r)
                        if k in (1, 2):
                            qk_rest(b + 1, k - 1)
                        if k == 3:
                            route_choose(b + 1)
                        if k == 4:
                            route_weigh(b + 1, 1 - r)
                            v(b + 1, 1 - r)
                        if k == 7:
                            v0_low(b + 1, 1 - r)
                    if not has_last and k == 1:
                        v0_low(b, r)
                    if not has_last:
                        if k in STATISTICS:
                            n = STATISTICS.index(k)
                            variance(LATER[n], LATER[n + 1])
                        if k == 7:
                            deviation(2 * NT, TILES, 4)
                    if has_last:
                        if k == 4:
                            divide(b - 1)
                        if k == 7:
                            add_out(b - 1)

            for_batches(dve, batch)
            split_h(B - 1, E - 1)
            weigh(B - 1, 1, E - 2)
            weigh(B - 1, 1, E - 1)
            divide(B - 1)
            add_out(B - 1)

        @block.tensor
        def _(pe):
            def mm3(dst, lhs, rhs, start=True, stop=True, **kw):
                pe.matmul(dst, lhs[0], rhs[0], start=start, stop=False, **kw)
                pe.matmul(dst, lhs[0], rhs[1], start=False, stop=False, **kw)
                return pe.matmul(dst, lhs[1], rhs[0], start=False, stop=stop, **kw)

            def warm_up(n):
                for _ in range(n):
                    pe.matmul(ps_s[:, 0, 0:P], ident[:, :], ident[:, :], start=True, stop=True)

            def xT_of(r, cols=slice(0, TB)):
                return xT_hi[:, r, cols], xT_lo[:, r, cols]

            def xT(b, r):
                pe.wait_ge(xn_ready, NT * (b + 1))
                wait_used(pe, sum_added, b - 1)
                wait_used(pe, gateT_ready, b)
                for t in range(NT):
                    last = pe.transpose(ps_t[:, t * P:(t + 1) * P], xn[:, r, t, :], ident[:, :])
                last.then_inc(xT_psum, 1)

            def r1(b, r):
                mm3(ps_t[:, 0:TB], (rw1_hi[:, :], rw1_lo[:, :]), xT_of(r)).then_inc(r1_psum, 1)

            def logits(b, r):
                pe.wait_ge(r1_ready, b + 1)
                for t in range(NT):
                    last = pe.matmul(ps_t[:, t * E:(t + 1) * E], r1T[:, r, t * P:(t + 1) * P], rw2_f[:, :],
                                     start=True, stop=True)
                last.then_inc(lg_psum, 1)

            def v(b, r):
                pe.wait_ge(lg_read, b + 1)
                w = [s[:, :, :].rearrange("p g c -> p (g c)") for s in (wv_hi, wv_lo)]
                for t in range(NT):
                    last = mm3(ps_t[:, t * TB:(t + 1) * TB], xT_of(r, slice(t * P, (t + 1) * P)), w)
                last.then_inc(v_psum, 1)

            def gate_T(b, r):
                pe.wait_ge(v_ready, b + 1)
                pe.wait_ge(gate_ready, b + 1)
                for t in range(NT):
                    last = pe.transpose(ps_t[0:E, t * P:(t + 1) * P], gate[:, r, t, :], ident[:, :])
                last.then_inc(gateT_psum, 1)

            def qk(b, r, g):
                if g == 0:
                    pe.wait_ge(xT_lo_done, b + 1)
                elif not isinstance(b, int) or b > 0:
                    pe.wait_ge(rest_done, b * NG + g)
                for m in range(2):
                    w = [s[:, m, g * P:(g + 1) * P] for s in (wqk_hi, wqk_lo)]
                    last = mm3(qk_psum(b, g)[:, m, :], w, xT_of(r))
                last.then_inc(q_psum, 1)

            def scores(b, r, k):
                wait_used(pe, square_done, b * PAIRS + k)
                for j in range(2):
                    h = 2 * k + j
                    pe.matmul(ps_s[:, j, TB:SW], k_stack[:, r, h, P:TB], q_stack[:, r, h, P:TB],
                              start=True, stop=True)
                    last = pe.matmul(ps_s[:, j, 0:TB], k_stack[:, r, h, 0:P], q_stack[:, r, h, :],
                                     start=True, stop=True)
                last.then_inc(s_psum, 1)

            def prefix_v(b, r):
                wait_used(pe, yn_ready, b)
                pe.wait_ge(v0_lo_done, b + 1)
                for a in range(2):
                    for n, part in enumerate((v0_hi, v0_lo)):
                        pe.matmul(ps_y[:, a, :], part[:, a * P:(a + 1) * P], before_r[:, :],
                                  start=(a == 0 and n == 0), stop=False, skip_group_check=True)
                    v1 = v_pad[:, r, 1, 4 * a:4 * (a + 1), :].rearrange("p g c -> p (g c)")
                    last = pe.matmul(ps_y[:, a, P:TB], v1, before[:, 0:P], start=False, stop=False, skip_group_check=True)
                last.then_inc(prefix_done, 1)

            def weigh_v(b, r, half):
                pe.wait_ge(mask_done, b * PAIRS + HALF * (half + 1))
                for j in range(2):
                    for t, cols in ((0, slice(0, TB)), (1, slice(TB, SW))):
                        for g in range(HALF):
                            k = HALF * half + g
                            if j == 0:
                                w = v_pad[:, r, t, k, 0:HD1]
                            else:
                                w = v_b[:, r, t, k, :]
                            dst = ps_y[VG * g:VG * g + HD1 * (j + 1), half, t * P:TB]
                            last = pe.matmul(dst, w, w_att[:, k, j, cols], start=False,
                                             stop=(half == 1 and j == 1 and t == 1), skip_group_check=True)
                last.then_inc(pv_done, 1)

            def hidden(b, r, e):
                wait_used(pe, silu_done, b * E + max(e - 1, 0))
                for c in range(NC):
                    w = [s[:, e, c * P:(c + 1) * P] for s in (ew1_hi, ew1_lo)]
                    last = mm3(ps_h[:, e % 2, c * TB:(c + 1) * TB], w, xT_of(r))
                last.then_inc(h_psum, 1)

            def expert_out(b, e):
                pe.wait_ge(h_lo_done, b * E + (e + 1))
                wait_used(pe, o_weighed, b * E + e)
                for c in range(NC):
                    w = [s[:, e * NC + c, :] for s in (ew2_hi, ew2_lo)]
                    last = mm3(ps_o[:, 0:TB], w, (h_hi[:, e % 2, c, :], h_lo[:, e % 2, c, :]),
                               start=(c == 0), stop=(c == NC - 1))
                last.then_inc(o_psum, 1)

            def num_T(b):
                pe.wait_ge(yn_ready, b + 1)
                pe.wait_ge(rest_done, b_groups(b))
                for t in range(NT):
                    for a in range(2):
                        last = pe.transpose(ps_q[:, t, a * P:(a + 1) * P], yn[:, a, t * P:(t + 1) * P], ident[:, :])
                last.then_inc(num_psum, 1)

            def b_groups(b):
                return min(NG * (b + 3), NG * B) if isinstance(b, int) else NG * (b + 3)

            def sum_out(b, r, last_batch):
                pe.wait_ge(o_added, (b + 1) * (E - 1))
                if not last_batch:
                    pe.wait_ge(gateT_ready, b + 3)
                for t in range(NT):
                    pe.matmul(ps_t[:, t * D:(t + 1) * D], oT[:, r, t * P:(t + 1) * P], ident[:, :],
                              start=(t == 0), stop=False, skip_group_check=True)
                pe.wait_ge(yT_ready, b + 1)
                for t in range(NT):
                    last = pe.matmul(ps_t[:, t * D:(t + 1) * D], yT[:, t * P:(t + 1) * P], wo_f[:, :],
                                     start=False, stop=(t == NT - 1), skip_group_check=True)
                last.then_inc(out_psum, 1)

            def y_T(b):
                pe.wait_ge(y_ready, b + 1)
                for t in range(NT):
                    last = pe.transpose(ps_q[:, 0, t * P:(t + 1) * P], y[:, t, :], ident[:, :])
                last.then_inc(yT_psum, 1)

            pe.wait_ge(const_step, 6)
            warm_up(9)
            xT(0, 0)
            pe.wait_ge(w_lo_done, 2)
            for g in range(NG):
                qk(0, 0, g)
            pe.wait_ge(w_lo_done, 3)
            r1(0, 0)
            warm_up(18)
            pe.wait_ge(small_in, 16 * SMALL_DMAS)
            logits(0, 0)
            pe.wait_ge(w_lo_done, 5)
            v(0, 0)
            warm_up(14)
            gate_T(0, 0)

            def batch(b, r, has_last, has_next):
                if not has_last:
                    pe.wait_ge(ew1_lo_done, 1)
                    hidden(b, r, 0)
                    xT(b + 1, 1 - r)
                for k in range(PAIRS):
                    if k % HALF == 0:
                        pe.wait_ge(stack_in[k // HALF], (b + 1) * (16 * STACK_DMAS))
                    scores(b, r, k)
                    if not has_last and k > 0:
                        pe.wait_ge(ew1_lo_done, k + 1)
                        hidden(b, r, k)
                    if k > 1:
                        if not has_last:
                            pe.wait_ge(ew2_lo_done, k - 1)
                        expert_out(b, k - 2)
                    elif has_last:
                        expert_out(b - 1, E - 2 + k)
                    if has_last:
                        hidden(b, r, k)
                    if k == 3:
                        prefix_v(b, r)
                    if has_last:
                        if k == 3:
                            num_T(b - 1)
                        if k == 5:
                            y_T(b - 1)
                    if k == 4:
                        weigh_v(b, r, 0)
                    if has_next:
                        if has_last and k == 0:
                            xT(b + 1, 1 - r)
                        if k in (1, 2):
                            qk(b + 1, 1 - r, k - 1)
                    if has_last and k == 0:
                        weigh_v(b - 1, 1 - r, 1)
                    if has_next:
                        if k == 1:
                            r1(b + 1, 1 - r)
                        if k == 2:
                            logits(b + 1, 1 - r)
                        if k == 3:
                            v(b + 1, 1 - r)
                        if k == 5:
                            gate_T(b + 1, 1 - r)
                    if has_last and k == 6:
                        sum_out(b - 1, 1 - r, not has_next)

            for_batches(pe, batch)
            expert_out(B - 1, E - 2)
            weigh_v(B - 1, 1, 1)
            expert_out(B - 1, E - 1)
            num_T(B - 1)
            y_T(B - 1)
            sum_out(B - 1, 1, True)


def kernel(**inputs):
    import numpy as np
    import concourse.bacc as bacc
    from concourse.bass_utils import run_bass_kernel_spmd

    g = {k: np.asarray(v) for k, v in inputs.items()}
    A, M = "L0_attn_", "L0_ffn_"
    E, _, HID = g[M + "ew1"].shape

    def heads_inside(w):
        return w.reshape(-1, 8, 16, w.shape[1]).transpose(0, 2, 1, 3).reshape(w.shape)

    laid = {
        "x": g[A + "hidden_states"],
        "wqT": heads_inside(g[A + "Wq"]).T, "wkT": heads_inside(g[A + "Wk"]).T, "wvT": g[A + "Wv"].T, "woT": g[A + "Wo"].T,
        "rw1": g[M + "rw1"], "rb1": g[M + "rb1"].reshape(-1, 1),
        "rw2": g[M + "rw2"], "rb2": g[M + "rb2"].reshape(1, -1),
        "ew1": g[M + "ew1"],
        "eb1": g[M + "eb1"].reshape(E * (HID // P), P).T,
        "ew2": g[M + "ew2"], "eb2": g[M + "eb2"].T,
    }
    nc = bacc.Bacc("TRN2", target_bir_lowering=False, num_devices=1)
    arrays, args = {}, []
    for name, a in laid.items():
        arrays[name] = np.ascontiguousarray(a)
        args.append(nc.dram_tensor(name, a.shape, mybir.dt.from_np(a.dtype), kind="ExternalInput").ap())
    args.append(nc.dram_tensor("out", laid["x"].shape, F32, kind="ExternalOutput").ap())
    fused_layer(nc, *args)
    r = run_bass_kernel_spmd(nc, [arrays], core_ids=[0])
    return r.results[0]["out"]
```
